# Optimizing a Trainium2 kernel written in Bass

```python
import numpy as np
import jax
import jax.numpy as jnp

def _softmax(x, axis=-1):
    return jax.nn.softmax(x, axis=axis)

def _gelu(x):
    return jax.nn.gelu(x, approximate=True)

def _silu(x):
    return jax.nn.silu(x)

def _sigmoid(x):
    return jax.nn.sigmoid(x)

def _layernorm(x, axis=-1, eps=1e-05):
    m = jnp.mean(x, axis=axis, keepdims=True)
    v = jnp.var(x, axis=axis, keepdims=True)
    return (x - m) / jnp.sqrt(v + eps)

def _scatter_add(tgt, idx, src, axis=0):
    return tgt.at[idx].add(src)

def _segment_sum(src, seg, n):
    return jax.ops.segment_sum(src, seg, n)
kernel_name = 'mk_seq_preln_d1_jaxref_r8_d2fe36'

def setup_inputs(seed: int=0):
    np.random.seed(seed)
    _w = jnp.asarray

    def _L0_attn_setup():
        import jax, jax.numpy as jnp
        import numpy as np
        EPS = float(np.finfo(np.float32).eps)
        THETA = 10000.0

        def rms_norm(x, weight):
            var = jnp.mean(jnp.square(x), axis=-1, keepdims=True)
            return x * jax.lax.rsqrt(var + EPS) * weight

        def rotate_half(x):
            x1 = x[..., ::2]
            x2 = x[..., 1::2]
            return jnp.stack((-x2, x1), axis=-1).reshape(x.shape)

        def apply_rope(t):
            d = t.shape[-1]
            n = t.shape[-2]
            inv_freq = 1.0 / THETA ** (jnp.arange(0, d, 2, dtype=jnp.float32) / d)
            freqs = jnp.arange(n, dtype=jnp.float32)[:, None] * inv_freq[None, :]
            freqs = jnp.repeat(freqs, 2, axis=-1)
            cos = jnp.cos(freqs).astype(t.dtype)
            sin = jnp.sin(freqs).astype(t.dtype)
            return t * cos + rotate_half(t) * sin
        key = jax.random.key(seed)
        k1, k2, k3, k4 = jax.random.split(key, 4)
        b, n, dim = (4, 256, 128)
        heads, dim_head, n_pm = (16, 64, 4)
        dim_inner = heads * dim_head
        return {'x': jax.random.normal(k1, (b, n, dim), dtype=jnp.float32), 'norm_weight': jnp.ones((dim,), dtype=jnp.float32), 'w_qkv': jax.random.normal(k2, (3 * dim_inner, dim), dtype=jnp.float32) * dim ** (-0.5), 'w_out': jax.random.normal(k3, (dim, dim_inner), dtype=jnp.float32) * dim_inner ** (-0.5), 'persist_mem': jax.random.normal(k4, (heads, n_pm, dim_head), dtype=jnp.float32)}
    _L0_attn_in = _L0_attn_setup()

    def _L0_ffn_setup():
        import jax, jax.numpy as jnp
        import numpy as np
        from jax import lax
        T, B, I, M, O = (32, 64, 128, 128, 128)

        def _xavier(key, shape):
            fan_out, fan_in = shape
            limit = float(np.sqrt(6.0 / (fan_in + fan_out)))
            return jax.random.uniform(key, shape, jnp.float32, -limit, limit)
        key = jax.random.key(seed)
        ks = jax.random.split(key, 9)
        x = jax.random.normal(ks[0], (T, B, I), jnp.float32)
        return {'x': x, 'wf': _xavier(ks[1], (M, I)), 'uf': _xavier(ks[2], (M, M)), 'bf': jnp.zeros((M,), jnp.float32), 'wi': _xavier(ks[3], (M, I)), 'ui': _xavier(ks[4], (M, M)), 'bi': jnp.zeros((M,), jnp.float32), 'wc': _xavier(ks[5], (M, I)), 'uc': _xavier(ks[6], (M, M)), 'bc': jnp.zeros((M,), jnp.float32), 'wo': _xavier(ks[7], (O, I)), 'uo': _xavier(ks[8], (O, M)), 'bo': jnp.zeros((O,), jnp.float32), 'in_c': jnp.zeros((M,), jnp.float32)}
    _L0_ffn_in = _L0_ffn_setup()
    _d = {'L0_attn_x': _L0_attn_in['x'], 'L0_attn_norm_weight': _L0_attn_in['norm_weight'], 'L0_attn_w_qkv': _L0_attn_in['w_qkv'], 'L0_attn_w_out': _L0_attn_in['w_out'], 'L0_attn_persist_mem': _L0_attn_in['persist_mem'], 'L0_ffn_wf': _L0_ffn_in['wf'], 'L0_ffn_uf': _L0_ffn_in['uf'], 'L0_ffn_bf': _L0_ffn_in['bf'], 'L0_ffn_wi': _L0_ffn_in['wi'], 'L0_ffn_ui': _L0_ffn_in['ui'], 'L0_ffn_bi': _L0_ffn_in['bi'], 'L0_ffn_wc': _L0_ffn_in['wc'], 'L0_ffn_uc': _L0_ffn_in['uc'], 'L0_ffn_bc': _L0_ffn_in['bc'], 'L0_ffn_wo': _L0_ffn_in['wo'], 'L0_ffn_uo': _L0_ffn_in['uo'], 'L0_ffn_bo': _L0_ffn_in['bo'], 'L0_ffn_in_c': _L0_ffn_in['in_c']}
    _x0 = _d['L0_attn_x']
    _d['L0_attn_x'] = jax.random.normal(jax.random.fold_in(jax.random.key(seed), 1), (32, 256, 128), dtype=_x0.dtype)
    del _x0
    return _d

def reference(L0_attn_x, L0_attn_norm_weight, L0_attn_w_qkv, L0_attn_w_out, L0_attn_persist_mem, L0_ffn_wf, L0_ffn_uf, L0_ffn_bf, L0_ffn_wi, L0_ffn_ui, L0_ffn_bi, L0_ffn_wc, L0_ffn_uc, L0_ffn_bc, L0_ffn_wo, L0_ffn_uo, L0_ffn_bo, L0_ffn_in_c):

    def _L0_attn_ref(x, norm_weight, w_qkv, w_out, persist_mem):
        import jax, jax.numpy as jnp
        import numpy as np
        EPS = float(np.finfo(np.float32).eps)
        THETA = 10000.0

        def rms_norm(x, weight):
            var = jnp.mean(jnp.square(x), axis=-1, keepdims=True)
            return x * jax.lax.rsqrt(var + EPS) * weight

        def rotate_half(x):
            x1 = x[..., ::2]
            x2 = x[..., 1::2]
            return jnp.stack((-x2, x1), axis=-1).reshape(x.shape)

        def apply_rope(t):
            d = t.shape[-1]
            n = t.shape[-2]
            inv_freq = 1.0 / THETA ** (jnp.arange(0, d, 2, dtype=jnp.float32) / d)
            freqs = jnp.arange(n, dtype=jnp.float32)[:, None] * inv_freq[None, :]
            freqs = jnp.repeat(freqs, 2, axis=-1)
            cos = jnp.cos(freqs).astype(t.dtype)
            sin = jnp.sin(freqs).astype(t.dtype)
            return t * cos + rotate_half(t) * sin
        b, n, _ = x.shape
        heads, n_pm, dim_head = persist_mem.shape
        h = rms_norm(x, norm_weight)
        qkv = h @ w_qkv.T
        q, k, v = jnp.split(qkv, 3, axis=-1)

        def split_heads(t):
            return t.reshape(b, n, heads, dim_head).transpose(0, 2, 1, 3)
        q, k, v = (split_heads(q), split_heads(k), split_heads(v))
        q = apply_rope(q)
        k = apply_rope(k)
        pm = jnp.broadcast_to(persist_mem[None], (b, heads, n_pm, dim_head))
        k = jnp.concatenate([pm, k], axis=2)
        v = jnp.concatenate([pm, v], axis=2)
        kv_len = k.shape[2]
        scale = dim_head ** (-0.5)
        scores = jnp.einsum('bhid,bhjd->bhij', q, k) * scale
        i = jnp.arange(n)[:, None]
        j = jnp.arange(kv_len)[None, :]
        causal = j <= i + (kv_len - n)
        scores = jnp.where(causal, scores, jnp.finfo(scores.dtype).min)
        attn = jax.nn.softmax(scores, axis=-1)
        out = jnp.einsum('bhij,bhjd->bhid', attn, v)
        out = out.transpose(0, 2, 1, 3).reshape(b, n, heads * dim_head)
        return out @ w_out.T

    def _L0_ffn_ref(x, wf, uf, bf, wi, ui, bi, wc, uc, bc, wo, uo, bo, in_c):
        import jax, jax.numpy as jnp
        import numpy as np
        from jax import lax
        T, B, I, M, O = (32, 64, 128, 128, 128)

        def _xavier(key, shape):
            fan_out, fan_in = shape
            limit = float(np.sqrt(6.0 / (fan_in + fan_out)))
            return jax.random.uniform(key, shape, jnp.float32, -limit, limit)
        batch = x.shape[1]
        c0 = jnp.broadcast_to(in_c, (batch, in_c.shape[0]))

        def step(c, xt):
            ft = jax.nn.sigmoid(xt @ wf.T + c @ uf.T + bf)
            it = jax.nn.sigmoid(xt @ wi.T + c @ ui.T + bi)
            gt = jnp.tanh(xt @ wc.T + c @ uc.T + bc)
            c = ft * c + it * gt
            return (c, None)
        c_final, _ = lax.scan(step, c0, x)
        h = jnp.tanh(jnp.einsum('tbi,oi->tbo', x, wo) + c_final @ uo.T + bo)
        return h
    x = L0_attn_x
    x = x + _L0_attn_ref(_layernorm(x, axis=-1), L0_attn_norm_weight, L0_attn_w_qkv, L0_attn_w_out, L0_attn_persist_mem)
    x = x + _L0_ffn_ref(_layernorm(x, axis=-1), L0_ffn_wf, L0_ffn_uf, L0_ffn_bf, L0_ffn_wi, L0_ffn_ui, L0_ffn_bi, L0_ffn_wc, L0_ffn_uc, L0_ffn_bc, L0_ffn_wo, L0_ffn_uo, L0_ffn_bo, L0_ffn_in_c)
    return x

_drawn_inputs = setup_inputs


def setup_inputs(seed=0):
    import zlib

    import numpy as np

    out = dict(_drawn_inputs(seed))
    spreads = {'L0_attn_norm_weight': (1.0, 0.2),
     'L0_ffn_bf': (0.0, 0.661),
     'L0_ffn_bi': (0.0, 0.677),
     'L0_ffn_bc': (0.0, 0.1),
     'L0_ffn_bo': (0.0, 0.1),
     'L0_ffn_in_c': (0.0, 0.8)}
    factors = {}
    for name, (base, spread) in spreads.items():
        noise = np.random.default_rng([zlib.crc32(name.encode()), seed]).standard_normal(out[name].shape)
        drawn = base * np.exp(spread * noise) if base else spread * noise
        out[name] = jnp.asarray(drawn.astype(out[name].dtype))
    for name, factor in factors.items():
        out[name] = (out[name] * factor).astype(out[name].dtype)
    return out
```

```python
import concourse.bass as bass
from concourse import mybir
from contextlib import ExitStack

NB, NT, D = 32, 256, 128
NH, DH, NPM = 16, 64, 4
DI = NH * DH
P = 128
NPAIR = NH // 2
QT = NT // P
NKEY = NT + NPM
NK2 = NKEY - 2 * P
KPAD = 3 * P
Q1 = P - NPM
Q2 = 2 * P - NPM
SCOL = NT + (NT - Q1) + (NT - Q2)
CHUNKS = [(0, 0, 0), (1, Q1, NT), (2, Q2, NT + NT - Q1)]
SW0 = P + NPM
WS = 64.0
RS = 256.0
EPS_LN = 1e-5
EPS_RMS = 1.1920928955078125e-07
GATES = 3

CONSTS = [("cos", NT), ("sin", NT), ("ident", P), ("mask_q", SW0), ("mask_k2", NT - Q2),
          ("sel_pair", NPAIR * P), ("sel_shift", NH * P), ("ones_sum", 4 * 32)]


def const_slices():
    at, out = 0, {}
    for name, n in CONSTS:
        out[name] = (at, at + n)
        at += n
    return out, at


def wait(eng, sem, count):
    if isinstance(count, int) and count <= 0:
        return
    eng.wait_ge(sem, count)


def build(nc, x, w_qkv_t, w_out_t, norm_w, pm_k, pm_v, ffn_w, ffn_b, bo_row, consts, out):
    f32, f16, bf16 = mybir.dt.float32, mybir.dt.float16, mybir.dt.bfloat16
    ALU = mybir.AluOpType
    ACT = mybir.ActivationFunctionType
    AX = mybir.AxisListType
    CS, NCONST = const_slices()

    ctx = ExitStack()
    with ctx:
        def sb(name, shape, dt):
            return ctx.enter_context(nc.sbuf_tensor(name, shape, dt))

        def sem(name):
            return ctx.enter_context(nc.semaphore(name))

        x_sb = sb("x_sb", [P, NB, QT * D], f32)
        h_hi = sb("h_hi", [P, NB, NKEY], f16)
        h_lo = sb("h_lo", [P, NB, NKEY], f16)
        h_end = sb("h_end", [P, 2, NB * NK2], f16)
        pre = sb("pre", [P, NB, QT * D], f32)
        pre_f = pre[:, :, :].rearrange("p b n -> p (b n)")
        w_raw = pre_f[:, 0:3 * DI]
        f_raw = pre_f[:, 3 * DI:3 * DI + 8 * P]
        c_raw = pre_f[:, 3 * DI + 8 * P:3 * DI + 8 * P + NCONST]
        assert 3 * DI + 8 * P + NCONST <= NB * QT * D
        w_hi = sb("w_hi", [P, 3 * DI], f16)
        w_lo = sb("w_lo", [P, 3 * DI], f16)
        f_hi = sb("f_hi", [P, 8, P], f16)
        f_lo = sb("f_lo", [P, 8, P], f16)
        wo_sb = sb("wo_sb", [P, NPAIR, D], f32)
        cos = sb("cos", [P, NT], f32)
        sin = sb("sin", [P, NT], f32)
        ident_f = sb("ident_f", [P, P], f32)
        ident_b = sb("ident_b", [P, P], bf16)
        mask_q = sb("mask_q", [P, SW0], bf16)
        mask_k2 = sb("mask_k2", [P, NT - Q2], bf16)
        sel_pair = sb("sel_pair", [P, NPAIR, P], f16)
        sel_shift = sb("sel_shift", [P, NH, P], bf16)
        ones_sum = sb("ones_sum", [P, 4, 32], f32)
        bias_raw = sb("bias_raw", [P, 4], f32)
        bias_half = sb("bias_half", [P, 2], f32)
        nw = sb("nw", [P, 1], f32)
        bo_sb = sb("bo_sb", [1, D], f32)
        bo_one = sb("bo_one", [1, P], f32)
        pmk_raw = sb("pmk_raw", [P, NPAIR * NPM], f32)
        stats = sb("stats", [P, NB * QT, 6], f32)
        st_a = sb("st_a", [P, NB * QT], f32)
        st_b = sb("st_b", [P, NB * QT], f32)
        st_c = sb("st_c", [P, NB * QT], f32)
        st_mean = sb("st_mean", [P, NB * QT], f32)
        st_r1 = sb("st_r1", [P, NB * QT], f32)
        st_r2 = sb("st_r2", [P, NB * QT], f32)
        expo = sb("expo", [P, NB * QT], f32)
        gate_col = sb("gate_col", [P, NPAIR], f32)
        eps = sb("eps", [P, QT], f32)
        xn0 = sb("xn0", [P, 2, QT * D], f32)
        rope_a = sb("rope_a", [P, 2, 2 * NT], f32)
        rope_b = sb("rope_b", [P, 2, 2 * NT], f32)
        q_hi = sb("q_hi", [P, NPAIR, NT], f16)
        q_lo = sb("q_lo", [P, NPAIR, NT], f16)
        k_hi = sb("k_hi", [P, NPAIR, KPAD], f16)
        k_lo = sb("k_lo", [P, NPAIR, KPAD], f16)
        v_sb = sb("v_sb", [P, 2, DI], f32)
        v2_sb = sb("v2_sb", [P, DI], f32)
        nmax = sb("nmax", [P, QT, NH], f32)
        nres = sb("nres", [P, QT, NH], f32)
        nsplit = sb("nsplit", [P, QT, 3, 32], bf16)
        nmax_t = sb("nmax_t", [96, NT], bf16)
        prob = sb("prob", [P, 4, 2, SCOL], f32)
        raw = sb("raw", [P, NPAIR, NT], f32)
        linv = sb("linv", [P, NT], f32)
        linv_hi = sb("linv_hi", [P, NT], f16)
        linv_lo = sb("linv_lo", [P, NT], f16)
        x1 = sb("x1", [P, QT * D], f32)
        sx = sb("sx", [P, QT, 6], f32)
        sx_a = sb("sx_a", [P, QT], f32)
        sx_b = sb("sx_b", [P, QT], f32)
        sx_c = sb("sx_c", [P, QT], f32)
        sx_mean = sb("sx_mean", [P, QT], f32)
        sx_r = sb("sx_r", [P, QT], f32)
        xn = sb("xn", [P, QT * D], f32)
        xt_hi = sb("xt_hi", [P, NT], f16)
        xt_lo = sb("xt_lo", [P, NT], f16)
        th = sb("th", [P, GATES, NT], f32)
        ga = sb("ga", [P, NT], f32)
        gb = sb("gb", [P, NT], f32)
        c2 = sb("c2", [P, NT], f32)
        c_hi = sb("c_hi", [P, NT], f16)
        c_lo = sb("c_lo", [P, NT], f16)
        cf = sb("cf", [P, QT * D], f32)
        v2_dram = nc.dram_tensor("v2_scratch", [P, DI], f32, kind="Internal").ap()

        bank = [ctx.enter_context(nc.psum_tensor(f"bank{i}", [P, 512], f32)) for i in range(8)]
        ps_proj = [bank[0], bank[1]]
        ps_st = [bank[2], bank[3]]
        ps_sm = bank[4]
        ps_pv = bank[5]
        ps_sum = bank[6]
        ps_misc = bank[7]

        S = {n: sem(n) for n in (
            "ld_x0 ld_x1 ld_x2 ld_x3 ld_w ld_c ld_small ld_wo "
            "casts_act casts_dve casts_pool stats_done rstd0 xn0_ready xt0_ready h_hi_done h_lo_done h_end_done v2_ready v2_copied v2_stored "
            "qk_proj qk_read rope_mul rope_sum q_hi_done q_lo_done sm_ready max_done split_done nmax_tr nmax_copied "
            "st_ready exp_done causal_done pv_ready raw_done sum_ready linv_done r_ready norm_done y_ready x1_done x1_saved "
            "v_ready v_done v_pm v_k2 sx_done sx_rstd xn_ready xt_ready xt_hi_done xt_lo_done gate_ready gate_read state_done "
            "cf_ready cf_done fin_sum fin_tanh fin_out stored "
            "dve_pro dve_a dve_b dve_c pool_pro pool_b act_pro").split()}

        DVE_A, DVE_B, DVE_C = 4, 9, 4
        SHUF = [i ^ 1 for i in range(32)]
        nchunk = 4
        xb = NB // nchunk
        ld_x = [S[f"ld_x{i}"] for i in range(nchunk)]
        x_d = x.rearrange("b (q p) d -> p b q d", p=P)
        out_d = out.rearrange("b (q p) d -> p b q d", p=P)

        def at3(t, b):
            return t[:, b, :] if isinstance(b, int) else t[:, bass.ds(b, 1), :].rearrange("p o n -> p (o n)")

        def at3s(t, b, lo, hi):
            return t[:, b, lo:hi] if isinstance(b, int) else t[:, bass.ds(b, 1), lo:hi].rearrange("p o n -> p (o n)")

        def iterations(eng, body):
            for j in (0, 1, 2):
                body(j, True, j >= 1, j >= 2)
            with eng.Fori(3, NB) as j:
                body(j, True, True, True)
            body(NB, False, True, True)
            body(NB + 1, False, False, True)

        block = ctx.enter_context(nc.Block())

        @block.sync
        def _(sp):
            for i in range(nchunk):
                sp.dma_start(x_sb[:, i * xb:(i + 1) * xb, :].rearrange("p b (q d) -> p b q d", q=QT),
                             x_d[:, i * xb:(i + 1) * xb, :, :]).then_inc(ld_x[i], 16)
            sp.dma_start(wo_sb[:, :, :], w_out_t.rearrange("(c p) d -> p c d", p=P)).then_inc(S["ld_wo"], 16)
            sp.wait_ge(S["v2_copied"], 2)
            sp.dma_start(v2_dram, raw[:, 0:4, :].rearrange("p c n -> p (c n)")).then_inc(S["v2_stored"], 16)
            sp.wait_ge(S["v2_stored"], 16)

            def body(j, a, b, c):
                if not a:
                    return
                wait(sp, S["pv_ready"], NPAIR * j)
                if isinstance(j, int) and j == 0:
                    sp.wait_ge(S["casts_pool"], 2)
                src = v2_dram[NPM * j:NPM * j + NPM, :] if isinstance(j, int) else v2_dram[bass.ds(j * NPM, NPM), :]
                sp.dma_start(v2_sb[0:NK2, :], src).then_inc(S["v_k2"], 16)
                sp.wait_ge(S["v_done"], 4 * j + 2)
                sp.dma_start(v_sb[0:NPM, 0, :], pm_v).then_inc(S["v_pm"], 16)

            iterations(nc.sync, body)
            for g in range(8):
                sp.wait_ge(S["fin_out"], g + 1)
                sp.dma_start(out_d[:, 4 * g:4 * g + 4, :, :],
                             x_sb[:, 4 * g:4 * g + 4, :].rearrange("p b (q d) -> p b q d", q=QT)).then_inc(S["stored"], 16)
            sp.wait_ge(S["stored"], 16 * 8)

        @block.gpsimd
        def _(pool):
            G = nc.gpsimd
            G.memset(expo[:, :], -0.5).then_inc(S["casts_pool"], 1)
            G.memset(v2_sb[:, :], 0.0).then_inc(S["casts_pool"], 1)
            G.memset(nsplit[:, :, :, :], 0.0).then_inc(S["casts_pool"], 1)
            G.memset(k_hi[:, :, :], 0.0).then_inc(S["casts_pool"], 1)
            G.memset(k_lo[:, :, :], 0.0).then_inc(S["casts_pool"], 1)
            G.memset(h_hi[:, :, 0:NPM], 0.0).then_inc(S["casts_pool"], 1)
            G.memset(h_lo[:, :, 0:NPM], 0.0).then_inc(S["casts_pool"], 1)
            G.memset(bo_one[:, :], WS).then_inc(S["casts_pool"], 1)
            G.memset(eps[:, :], EPS_LN).then_inc(S["casts_pool"], 1)

            chain = [0]

            def link(ins):
                chain[0] += 1
                ins.then_inc(S["pool_pro"], 1)
                pool.wait_ge(S["pool_pro"], chain[0])

            pool.wait_ge(S["casts_pool"], 1)
            pool.wait_ge(S["stats_done"], 1)
            link(G.tensor_scalar(st_a[:, :], st_b[:, :], EPS_LN, None, ALU.add))
            link(G.tensor_tensor(st_r1[:, :], st_a[:, :], expo[:, :], ALU.pow))
            link(G.tensor_tensor(st_a[:, :], st_r1[:, :], st_r1[:, :], ALU.mult))
            link(G.tensor_tensor(st_c[:, :], st_a[:, :], st_b[:, :], ALU.mult))
            link(G.tensor_scalar(st_c[:, :], st_c[:, :], EPS_RMS, None, ALU.add))
            link(G.tensor_tensor(st_r2[:, :], st_c[:, :], expo[:, :], ALU.pow))
            G.tensor_tensor(st_r1[:, :], st_r1[:, :], st_r2[:, :], ALU.mult).then_inc(S["rstd0"], 1)

            def body(j, a, b, c):
                bj = j - 1
                for s in range(NPAIR):
                    slot = s % 2
                    if a:
                        pool.wait_ge(S["qk_read"], NPAIR * j + s + 1)
                        rb = rope_b[:, slot, :].rearrange("p (u n) -> p u n", u=2)
                        sn = sin[:, :].unsqueeze(1).to_broadcast([P, 2, NT])
                        G.tensor_tensor(rb, rb, sn, ALU.mult).then_inc(S["rope_mul"], 1)
                    if b:
                        pool.wait_ge(S["exp_done"], NH * bj + 2 * s + 2)
                        G.tensor_tensor(gate_col[:, s:s + 1], expo[:, 0:1], expo[:, 0:1], ALU.mult)
                        c0 = prob[:, s % 4, :, 0:P]
                        c1 = prob[:, s % 4, :, NT:NT + P]
                        G.affine_select(out=c0, in_=c0, compare_op=ALU.is_ge, fill=0.0, base=NPM,
                                        pattern=[[0, 2], [1, P]], channel_multiplier=-1)
                        G.affine_select(out=c1, in_=c1, compare_op=ALU.is_ge, fill=0.0, base=0,
                                        pattern=[[0, 2], [1, P]], channel_multiplier=-1).then_inc(S["causal_done"], 1)
                    if a:
                        pool.wait_ge(S["rope_mul"], NPAIR * j + s + 1)
                        G.tensor_tensor(rope_a[:, slot, :], rope_a[:, slot, :], rope_b[:, slot, :],
                                        ALU.add).then_inc(S["rope_sum"], 1)
                if b:
                    pool.wait_ge(S["sx_done"], bj + 1)
                    G.tensor_tensor(sx_b[:, :], sx_a[:, :], eps[:, :], ALU.add).then_inc(S["pool_b"], 1)
                    pool.wait_ge(S["pool_b"], bj + 1)
                    G.tensor_tensor(sx_r[:, :], sx_b[:, :], expo[:, 0:QT], ALU.pow).then_inc(S["sx_rstd"], 1)
                    G.tensor_copy(at3(x_sb, bj), x1[:, :]).then_inc(S["x1_saved"], 1)

            iterations(nc.gpsimd, body)

        @block.scalar
        def _(act):
            A = nc.scalar
            act.dma_start(w_raw, w_qkv_t).then_inc(S["ld_w"], 16)
            act.dma_start(c_raw, consts).then_inc(S["ld_c"], 16)
            act.dma_start(f_raw, ffn_w).then_inc(S["ld_small"], 16)
            act.dma_start(bias_raw[:, :], ffn_b).then_inc(S["ld_small"], 16)
            act.dma_start(nw[:, :], norm_w).then_inc(S["ld_small"], 16)
            act.dma_start(bo_sb[:, :], bo_row).then_inc(S["ld_small"], 16)
            act.dma_start(pmk_raw[:, :], pm_k).then_inc(S["ld_small"], 16)
            act.wait_ge(S["ld_w"], 16)
            A.activation(w_hi[:, :], w_raw, ACT.Copy, scale=WS).then_inc(S["casts_act"], 1)
            act.wait_ge(S["ld_small"], 80)
            fr = f_raw.rearrange("p (g n) -> p g n", g=8)
            A.activation(f_hi[:, 0:4, :], fr[:, 0:4, :], ACT.Copy, scale=WS).then_inc(S["casts_act"], 1)
            A.activation(f_hi[:, 4:8, :], fr[:, 4:8, :], ACT.Copy, scale=WS / 2).then_inc(S["casts_act"], 1)
            A.activation(bias_half[:, :], bias_raw[:, 0:2], ACT.Copy, scale=0.5).then_inc(S["casts_act"], 1)
            act.wait_ge(S["ld_c"], 16)

            def const(name):
                return c_raw[:, CS[name][0]:CS[name][1]]

            A.copy(cos[:, :], const("cos")).then_inc(S["casts_act"], 1)
            A.copy(sin[:, :], const("sin")).then_inc(S["casts_act"], 1)
            A.copy(ident_f[:, :], const("ident")).then_inc(S["casts_act"], 1)
            A.copy(ident_b[:, :], const("ident")).then_inc(S["casts_act"], 1)
            A.copy(mask_q[:, :], const("mask_q")).then_inc(S["casts_act"], 1)
            A.copy(mask_k2[:, :], const("mask_k2")).then_inc(S["casts_act"], 1)
            A.copy(sel_pair[:, :, :].rearrange("p c n -> p (c n)"), const("sel_pair")).then_inc(S["casts_act"], 1)
            A.copy(sel_shift[:, :, :].rearrange("p c n -> p (c n)"), const("sel_shift")).then_inc(S["casts_act"], 1)
            A.copy(ones_sum[:, :, :].rearrange("p c n -> p (c n)"), const("ones_sum")).then_inc(S["casts_act"], 1)

            with nc.scalar.Fori(0, NB // 2) as i:
                for u in range(2):
                    b = i * 2 + u
                    act.wait_ge(S["xt0_ready"], b + 1)
                    A.activation(at3s(h_hi, b, NPM, NKEY), bank[u][:, 0:NT], ACT.Copy,
                                 scale=nw[:, :]).then_inc(S["h_hi_done"], 1)
            for u in range(2):
                act.wait_ge(S["v2_ready"], u + 1)
                A.activation(raw[:, 2 * u:2 * u + 2, :].rearrange("p c n -> p (c n)"), bank[2 + u][:, :], ACT.Copy,
                             scale=1.0 / WS).then_inc(S["v2_copied"], 1)

            def hi(j, s):
                act.wait_ge(S["rope_sum"], NPAIR * j + s + 1)
                wait(act, S["st_ready"], NH * (j - 1) + 2 * s + 2)
                if isinstance(j, int) and j == 0 and s == 0:
                    act.wait_ge(S["casts_pool"], 5)
                A.activation(q_hi[:, s, :], rope_a[:, s % 2, 0:NT], ACT.Copy)
                A.activation(k_hi[:, s, NPM:NKEY], rope_a[:, s % 2, NT:2 * NT], ACT.Copy).then_inc(S["q_hi_done"], 1)

            def exp(bj, h):
                s = h // 2
                act.wait_ge(S["st_ready"], NH * bj + h + 1)
                if h % 2 == 0:
                    wait(act, S["sum_ready"], 4 * bj + (s - 4) // 2 + 1)
                A.activation(prob[:, s % 4, h % 2, :], ps_st[h % 2][:, 0:SCOL], ACT.Exp,
                             scale=DH ** -0.5).then_inc(S["exp_done"], 1)

            def raw_copy(bj, s):
                act.wait_ge(S["pv_ready"], NPAIR * bj + s + 1)
                if s == 0:
                    wait(act, S["y_ready"], bj)
                if isinstance(bj, int) and bj == 0 and s == 0:
                    act.wait_ge(S["v2_stored"], 16)
                A.activation(raw[:, s, :], ps_pv[:, 0:NT], ACT.Copy, scale=1.0 / RS).then_inc(S["raw_done"], 1)

            def body(j, a, b, c):
                bj, cj = j - 1, j - 2
                for s in range(NPAIR):
                    if b:
                        exp(bj, 2 * s)
                    if a and s >= 1:
                        hi(j, s - 1)
                    if b:
                        exp(bj, 2 * s + 1)
                    if b and s >= 1:
                        raw_copy(bj, s - 1)
                    if c and s == 1:
                        act.wait_ge(S["xt_ready"], cj + 1)
                        wait(act, S["gate_ready"], 2 * cj)
                        A.activation(xt_hi[:, :], ps_misc[:, 0:NT], ACT.Copy).then_inc(S["xt_hi_done"], 1)
                    if c and s == 3:
                        act.wait_ge(S["gate_ready"], 2 * cj + 1)
                        wait(act, S["state_done"], cj)
                        A.activation(th[:, 0, :], ps_proj[0][:, 0:NT], ACT.Tanh, bias=bias_half[:, 0:1],
                                     scale=0.5 / WS)
                        A.activation(th[:, 1, :], ps_proj[0][:, NT:2 * NT], ACT.Tanh, bias=bias_half[:, 1:2],
                                     scale=0.5 / WS).then_inc(S["gate_read"], 1)
                        act.wait_ge(S["gate_ready"], 2 * cj + 2)
                        A.activation(th[:, 2, :], ps_proj[1][:, 0:NT], ACT.Tanh, bias=bias_raw[:, 2:3],
                                     scale=1.0 / WS)
                        A.activation(at3(pre, cj), ps_proj[1][:, NT:2 * NT], ACT.Copy).then_inc(S["gate_read"], 1)
                if a:
                    hi(j, NPAIR - 1)
                if b:
                    raw_copy(bj, NPAIR - 1)
                if a:
                    for n in range(4):
                        act.wait_ge(S["v_ready"], 4 * j + n + 1)
                        A.activation(v_sb[:, n // 2, (n % 2) * 512:(n % 2) * 512 + 512], ps_proj[n % 2][:, :], ACT.Copy,
                                     scale=1.0 / WS).then_inc(S["v_done"], 1)
                    act.wait_ge(S["nmax_tr"], j + 1)
                    A.copy(nmax_t[:, :], ps_sum[:, :].bitcast(bf16)[0:96, 0:NT]).then_inc(S["nmax_copied"], 1)

            iterations(nc.scalar, body)

            act.wait_ge(S["cf_ready"], 1)
            A.copy(cf[:, :], ps_misc[:, 0:NT]).then_inc(S["cf_done"], 1)
            for g in range(8):
                act.wait_ge(S["fin_sum"], g + 1)
                v = pre[:, 4 * g:4 * g + 4, :]
                A.activation(v, v, ACT.Tanh, scale=1.0 / WS).then_inc(S["fin_tanh"], 1)

        @block.vector
        def _(dve):
            V = nc.vector
            chain = [0]

            def link(ins):
                chain[0] += 1
                ins.then_inc(S["dve_pro"], 1)
                dve.wait_ge(S["dve_pro"], chain[0])

            dve.wait_ge(S["casts_act"], 1)
            V.scalar_tensor_tensor(w_lo[:, :], w_raw, WS, w_hi[:, :], ALU.mult, ALU.subtract).then_inc(S["casts_dve"], 1)
            dve.wait_ge(S["casts_act"], 3)
            fr = f_raw.rearrange("p (g n) -> p g n", g=8)
            V.scalar_tensor_tensor(f_lo[:, 0:4, :], fr[:, 0:4, :], WS, f_hi[:, 0:4, :], ALU.mult,
                                   ALU.subtract).then_inc(S["casts_dve"], 1)
            V.scalar_tensor_tensor(f_lo[:, 4:8, :], fr[:, 4:8, :], WS / 2, f_hi[:, 4:8, :], ALU.mult,
                                   ALU.subtract).then_inc(S["casts_dve"], 1)
            dve.wait_ge(S["casts_pool"], 5)
            pk = pmk_raw[:, :].rearrange("p (c n) -> p c n", c=NPAIR)
            link(V.tensor_copy(k_hi[:, :, 0:NPM], pk))
            V.tensor_tensor(k_lo[:, :, 0:NPM], pk, k_hi[:, :, 0:NPM], ALU.subtract).then_inc(S["casts_dve"], 1)
            link(V.memset(c2[:, :], 2.0))
            link(V.tensor_scalar(c2[:, :], c2[:, :], bias_raw[:, 3:4], None, ALU.mult))
            link(V.tensor_copy(c_hi[:, :], c2[:, :]))
            link(V.tensor_tensor(c_lo[:, :], c2[:, :], c_hi[:, :], ALU.subtract))

            for i in range(nchunk):
                dve.wait_ge(ld_x[i], 16)
                with nc.vector.Fori(i * xb * QT, (i + 1) * xb * QT) as t:
                    xt = x_sb[:, :, :].rearrange("p b (q d) -> p (b q) d", q=QT)
                    V.bn_stats(stats[:, bass.ds(t, 1), :].rearrange("p o n -> p (o n)"),
                               xt[:, bass.ds(t, 1), :].rearrange("p o n -> p (o n)"))
            link(V.memset(gb[:, :], 0.0))

            def moments(src, diff, tmp, mean, var, lnk):
                lnk(V.tensor_tensor(diff, src[:, :, 1], src[:, :, 4], ALU.subtract))
                lnk(V.tensor_tensor(mean, src[:, :, 1], src[:, :, 4], ALU.add))
                lnk(V.tensor_tensor(tmp, src[:, :, 2], src[:, :, 5], ALU.add))
                lnk(V.scalar_tensor_tensor(diff, diff, 0.25, diff, ALU.mult, ALU.mult))
                lnk(V.tensor_scalar(mean, mean, 0.5, None, ALU.mult))
                return V.scalar_tensor_tensor(var, tmp, 1.0 / D, diff, ALU.mult, ALU.add)

            moments(stats[:, :, :], st_a[:, :], st_c[:, :], st_mean[:, :], st_b[:, :], link).then_inc(S["stats_done"], 1)

            dve.wait_ge(S["rstd0"], 1)

            def xn0_of(b, u, q):
                t = b * QT + q
                mean = st_mean[:, bass.ds(t, 1)]
                r = st_r1[:, bass.ds(t, 1)]
                xin = x_sb[:, bass.ds(b, 1), q * D:(q + 1) * D].rearrange("p o n -> p (o n)")
                return V.tensor_scalar(xn0[:, u, q * D:(q + 1) * D], xin, mean, r, ALU.subtract, ALU.mult)

            with nc.vector.Fori(0, NB // 2) as i:
                for u in range(2):
                    b = i * 2 + u
                    dve.wait_ge(S["xt0_ready"], b - u)
                    xn0_of(b, u, 0)
                    xn0_of(b, u, 1).then_inc(S["xn0_ready"], 1)
                for u in range(2):
                    b = i * 2 + u
                    dve.wait_ge(S["h_hi_done"], b + 1)
                    V.scalar_tensor_tensor(at3s(h_lo, b, NPM, NKEY), bank[u][:, 0:NT], nw[:, :],
                                           at3s(h_hi, b, NPM, NKEY), ALU.mult, ALU.subtract).then_inc(S["h_lo_done"], 1)

            dve.wait_ge(S["h_lo_done"], NB)
            for u, h in enumerate((h_hi, h_lo)):
                V.tensor_copy(h_end[:, u, :].rearrange("p (b n) -> p b n", n=NK2),
                              h[:, :, 2 * P:NKEY]).then_inc(S["h_end_done"], 1)

            def body(j, a, b, c):
                bj, cj = j - 1, j - 2
                ka, kb, kc = [0], [0], [0]

                def link_a(ins):
                    ka[0] += 1
                    ins.then_inc(S["dve_a"], 1)
                    dve.wait_ge(S["dve_a"], DVE_A * j + ka[0])

                def link_b(ins):
                    kb[0] += 1
                    ins.then_inc(S["dve_b"], 1)
                    dve.wait_ge(S["dve_b"], DVE_B * bj + kb[0])

                def link_c(ins):
                    kc[0] += 1
                    ins.then_inc(S["dve_c"], 1)
                    dve.wait_ge(S["dve_c"], DVE_C * cj + kc[0])

                def low(s):
                    dve.wait_ge(S["q_hi_done"], NPAIR * j + s + 1)
                    V.tensor_tensor(q_lo[:, s, :], rope_a[:, s % 2, 0:NT], q_hi[:, s, :], ALU.subtract)
                    V.tensor_tensor(k_lo[:, s, NPM:NKEY], rope_a[:, s % 2, NT:2 * NT], k_hi[:, s, NPM:NKEY],
                                    ALU.subtract).then_inc(S["q_lo_done"], 1)

                def maxima(h):
                    dve.wait_ge(S["sm_ready"], NH * j + h + 1)
                    V.tensor_reduce(nmax[:, 0, h:h + 1], ps_sm[:, 0:SW0], AX.X, ALU.max, negate=True)
                    V.tensor_reduce(nmax[:, 1, h:h + 1], ps_sm[:, SW0:SW0 + NKEY], AX.X, ALU.max,
                                    negate=True).then_inc(S["max_done"], 1)

                for s in range(NPAIR):
                    if a:
                        dve.wait_ge(S["qk_proj"], NPAIR * j + s + 1)
                        wait(dve, S["q_lo_done"], NPAIR * j + s - 1)
                        qk = ps_proj[s % 2][:, :].rearrange("p (u n) -> p u n", u=2)
                        cs = cos[:, :].unsqueeze(1).to_broadcast([P, 2, NT])
                        V.tensor_tensor(rope_a[:, s % 2, :].rearrange("p (u n) -> p u n", u=2), qk, cs, ALU.mult)
                        V.stream_shuffle(rope_b[:, s % 2, :], ps_proj[s % 2][:, :], SHUF).then_inc(S["qk_read"], 1)
                        if s >= 2:
                            maxima(2 * s - 4)
                            maxima(2 * s - 3)
                        if s >= 1:
                            low(s - 1)
                    if c and s == 0:
                        dve.wait_ge(S["sx_rstd"], cj + 1)
                        wait(dve, S["xt_ready"], cj)
                        for q in range(QT):
                            last = V.tensor_scalar(xn[:, q * D:(q + 1) * D], x1[:, q * D:(q + 1) * D],
                                                   sx_mean[:, q:q + 1], sx_r[:, q:q + 1], ALU.subtract, ALU.mult)
                        last.then_inc(S["xn_ready"], 1)
                    if c and s == 1:
                        dve.wait_ge(S["xt_hi_done"], cj + 1)
                        V.tensor_tensor(xt_lo[:, :], ps_misc[:, 0:NT], xt_hi[:, :], ALU.subtract).then_inc(S["xt_lo_done"], 1)
                    if c and s == 4:
                        dve.wait_ge(S["gate_read"], 2 * cj + 2)
                        link_c(V.scalar_tensor_tensor(ga[:, :], th[:, 0, :], 1.0, c2[:, :], ALU.add, ALU.mult))
                        link_c(V.scalar_tensor_tensor(gb[:, :], th[:, 1, :], 1.0, th[:, 2, :], ALU.add, ALU.mult))
                        link_c(V.scalar_tensor_tensor(c2[:, :], ga[:, :], 0.5, gb[:, :], ALU.mult, ALU.add))
                        link_c(V.tensor_copy(c_hi[:, :], c2[:, :]))
                        V.tensor_tensor(c_lo[:, :], c2[:, :], c_hi[:, :], ALU.subtract).then_inc(S["state_done"], 1)
                if a:
                    low(NPAIR - 1)
                    maxima(12)
                    maxima(13)
                if b:
                    dve.wait_ge(S["sum_ready"], 4 * bj + 4)
                    link_b(V.reciprocal(linv[:, :], ps_sum[:, 0:NT]))
                    link_b(V.tensor_scalar(linv[:, :], linv[:, :], RS, None, ALU.mult))
                    link_b(V.tensor_copy(linv_hi[:, :], linv[:, :]))
                    V.tensor_tensor(linv_lo[:, :], linv[:, :], linv_hi[:, :], ALU.subtract).then_inc(S["linv_done"], 1)
                if a:
                    maxima(14)
                    maxima(15)
                    dve.wait_ge(S["max_done"], NH * j + NH)
                    wait(dve, S["nmax_tr"], j)
                    if isinstance(j, int) and j == 0:
                        dve.wait_ge(S["casts_pool"], 3)
                    link_a(V.tensor_copy(nsplit[:, :, 0, 0:NH], nmax[:, :, :]))
                    link_a(V.tensor_tensor(nres[:, :, :], nmax[:, :, :], nsplit[:, :, 0, 0:NH], ALU.subtract))
                    link_a(V.tensor_copy(nsplit[:, :, 1, 0:NH], nres[:, :, :]))
                    link_a(V.tensor_tensor(nres[:, :, :], nres[:, :, :], nsplit[:, :, 1, 0:NH], ALU.subtract))
                    V.tensor_copy(nsplit[:, :, 2, 0:NH], nres[:, :, :]).then_inc(S["split_done"], 1)
                if b:
                    dve.wait_ge(S["raw_done"], NPAIR * bj + NPAIR)
                    for n in range(4):
                        dve.wait_ge(S["r_ready"], 4 * bj + n + 1)
                        r = (ps_misc, ps_sum)[n % 2]
                        o = raw[:, 2 * n:2 * n + 2, :].rearrange("p c n -> p (c n)")
                        V.tensor_tensor(o, r[:, :], o, ALU.mult).then_inc(S["norm_done"], 1)
                    dve.wait_ge(S["y_ready"], bj + 1)
                    wait(dve, S["x1_saved"], bj)
                    V.tensor_tensor(x1[:, :], ps_misc[:, 0:QT * D], at3(x_sb, bj), ALU.add).then_inc(S["x1_done"], 1)
                    dve.wait_ge(S["x1_done"], bj + 1)
                    V.bn_stats(sx[:, 0, :], x1[:, 0:D])
                    link_b(V.bn_stats(sx[:, 1, :], x1[:, D:2 * D]))
                    moments(sx[:, :, :], sx_b[:, :], sx_c[:, :], sx_mean[:, :], sx_a[:, :], link_b).then_inc(S["sx_done"], 1)
                assert not a or ka[0] == DVE_A
                assert not b or kb[0] == DVE_B, kb
                assert not c or kc[0] == DVE_C

            iterations(nc.vector, body)

            dve.wait_ge(S["cf_done"], 1)

            def fin_add(g):
                v = pre[:, 4 * g:4 * g + 4, :]
                V.tensor_tensor(v, v, cf[:, :].unsqueeze(1).to_broadcast([P, 4, QT * D]), ALU.add).then_inc(S["fin_sum"], 1)

            def fin_res(g):
                dve.wait_ge(S["fin_tanh"], g + 1)
                v = pre[:, 4 * g:4 * g + 4, :]
                o = x_sb[:, 4 * g:4 * g + 4, :]
                V.tensor_tensor(o, o, v, ALU.add).then_inc(S["fin_out"], 1)

            dve.wait_ge(S["x1_saved"], NB)
            fin_add(0)
            for g in range(1, 8):
                fin_add(g)
                fin_res(g - 1)
            fin_res(7)

        @block.tensor
        def _(pe):
            T = nc.tensor
            pe.wait_ge(S["casts_act"], 13)
            with nc.tensor.Fori(0, NB // 2) as i:
                for u in range(2):
                    b = i * 2 + u
                    pe.wait_ge(S["xn0_ready"], b + 1)
                    pe.wait_ge(S["h_lo_done"], b - u)
                    for q in range(QT):
                        last = T.transpose(bank[u][:, q * P:(q + 1) * P], xn0[:, u, q * D:(q + 1) * D], ident_f[:, :])
                    last.then_inc(S["xt0_ready"], 1)
            pe.wait_ge(S["h_lo_done"], NB)
            pe.wait_ge(S["h_end_done"], 2)
            pe.wait_ge(S["casts_dve"], 4)
            pe.wait_ge(S["casts_pool"], 8)
            SPLIT = [(0, 0), (0, 1), (1, 0)]
            H, W, FW = (h_hi, h_lo), (w_hi, w_lo), (f_hi, f_lo)
            for u in range(2):
                for i, (p, q) in enumerate(SPLIT):
                    last = T.matmul(bank[2 + u][:, :], h_end[:, p, :], W[q][:, 2 * DI + u * 512:2 * DI + u * 512 + 512],
                                    start=(i == 0), stop=(i == 2))
                last.then_inc(S["v2_ready"], 1)
            pe.wait_ge(S["v2_copied"], 2)
            pe.wait_ge(S["ld_wo"], 16)

            def project(j, s):
                if s >= 2:
                    pe.wait_ge(S["qk_read"], NPAIR * j + s - 1)
                else:
                    wait(pe, S["v_done"], 4 * j - 1 + s)
                for u in range(2):
                    col = u * DI + s * P
                    for i, (p, q) in enumerate(SPLIT):
                        last = T.matmul(ps_proj[s % 2][:, u * NT:(u + 1) * NT], W[q][:, col:col + P],
                                        at3s(H[p], j, NPM, NKEY), start=(i == 0), stop=(i == 2))
                last.then_inc(S["qk_proj"], 1)

            def values(j):
                for n in range(4):
                    if n < 2:
                        pe.wait_ge(S["qk_read"], NPAIR * j + 7 + n)
                    else:
                        pe.wait_ge(S["v_done"], 4 * j + n - 1)
                    kc, col = n // 2, 2 * DI + (n % 2) * 512
                    for i, (p, q) in enumerate(SPLIT):
                        last = T.matmul(ps_proj[n % 2][:, :], at3s(H[p], j, kc * P, kc * P + P), W[q][:, col:col + 512],
                                        start=(i == 0), stop=(i == 2))
                    last.then_inc(S["v_ready"], 1)

            def scores_for_max(j, h):
                s, e = h // 2, h % 2
                if e == 0:
                    pe.wait_ge(S["q_hi_done"], NPAIR * j + s + 1)
                wait(pe, S["max_done"], NH * j + h)
                rows = slice(64 * e, 64 * e + 64)
                for q, c0, n in ((0, 0, SW0), (1, SW0, NKEY)):
                    T.matmul(ps_sm[:, c0:c0 + n], q_hi[rows, s, q * P:(q + 1) * P], k_hi[rows, s, 0:n],
                             start=True, stop=False)
                    last = T.matmul(ps_sm[:, c0 + n - SW0:c0 + n], ident_b[:, :], mask_q[:, :], start=False, stop=True)
                last.then_inc(S["sm_ready"], 1)

            def transpose_max(j):
                pe.wait_ge(S["split_done"], j + 1)
                wait(pe, S["norm_done"], 4 * j)
                o = ps_sum[:, :].bitcast(bf16)
                for q in range(QT):
                    last = T.transpose(o[0:96, q * P:(q + 1) * P], nsplit[:, q, :, :].rearrange("p a b -> p (a b)"),
                                       ident_b[:, :])
                last.then_inc(S["nmax_tr"], 1)

            def scores_t(bj, h):
                s, e = h // 2, h % 2
                if h == 0:
                    pe.wait_ge(S["nmax_copied"], bj + 1)
                if e == 0:
                    pe.wait_ge(S["q_lo_done"], NPAIR * bj + s + 1)
                wait(pe, S["exp_done"], NH * bj + h - 1)
                rows = slice(64 * e, 64 * e + 64)
                ps = ps_st[e]
                for kc, q0, c0 in CHUNKS:
                    o = ps[:, c0:c0 + NT - q0]
                    for i, (kk, qq) in enumerate(((k_hi, q_hi), (k_hi, q_lo), (k_lo, q_hi))):
                        T.matmul(o, kk[rows, s, kc * P:(kc + 1) * P], qq[rows, s, q0:NT], start=(i == 0), stop=False)
                    last = T.matmul(o, sel_shift[0:96, h, :], nmax_t[:, q0:NT], start=False, stop=(kc < 2))
                last = T.matmul(o, ident_b[:, :], mask_k2[:, :], start=False, stop=True)
                last.then_inc(S["st_ready"], 1)

            def attend(bj, s):
                pe.wait_ge(S["causal_done"], NPAIR * bj + s + 1)
                wait(pe, S["raw_done"], NPAIR * bj + s)
                if s == 0:
                    pe.wait_ge(S["v_done"], 4 * bj + 4)
                    pe.wait_ge(S["v_pm"], 16 * bj + 16)
                    pe.wait_ge(S["v_k2"], 16 * bj + 16)
                for kc, q0, c0 in CHUNKS:
                    for e in range(2):
                        col = (2 * s + e) * DH
                        v = v_sb[:, kc, col:col + DH] if kc < 2 else v2_sb[:, col:col + DH]
                        last = T.matmul(ps_pv[64 * e:64 * e + 64, q0:NT], v, prob[:, s % 4, e, c0:c0 + NT - q0],
                                        start=(kc == 0), stop=(kc == 2))
                last.then_inc(S["pv_ready"], 1)

            def sums(bj, g):
                if g == 0:
                    pe.wait_ge(S["nmax_copied"], bj + 1)
                for kc, q0, c0 in CHUNKS:
                    for r in range(4):
                        last = T.matmul(ps_sum[32 * r:32 * r + 32, q0:NT], ones_sum[:, g, :],
                                        prob[:, (2 * g + r // 2) % 4, r % 2, c0:c0 + NT - q0],
                                        start=(g == 0 and kc == 0), stop=(g == 3 and kc == 2))
                last.then_inc(S["sum_ready"], 1)

            def spread(bj):
                pe.wait_ge(S["linv_done"], bj + 1)
                for n in range(4):
                    if n >= 2:
                        pe.wait_ge(S["norm_done"], 4 * bj + n - 1)
                    r = (ps_misc, ps_sum)[n % 2]
                    for u in range(2):
                        T.matmul(r[:, u * NT:(u + 1) * NT], sel_pair[:, 2 * n + u, :], linv_hi[:, :], start=True, stop=False)
                        last = T.matmul(r[:, u * NT:(u + 1) * NT], sel_pair[:, 2 * n + u, :], linv_lo[:, :],
                                        start=False, stop=True)
                    last.then_inc(S["r_ready"], 1)

            def project_out(bj):
                pe.wait_ge(S["norm_done"], 4 * bj + 4)
                for q in range(QT):
                    for s in range(NPAIR):
                        last = T.matmul(ps_misc[:, q * D:(q + 1) * D], raw[:, s, q * P:(q + 1) * P], wo_sb[:, s, :],
                                        start=(s == 0), stop=(s == NPAIR - 1))
                last.then_inc(S["y_ready"], 1)

            def transpose_xn(cj):
                pe.wait_ge(S["xn_ready"], cj + 1)
                for q in range(QT):
                    last = T.transpose(ps_misc[:, q * P:(q + 1) * P], xn[:, q * D:(q + 1) * D], ident_f[:, :])
                last.then_inc(S["xt_ready"], 1)

            def gates(j, cj, a):
                pe.wait_ge(S["xt_lo_done"], cj + 1)
                wait(pe, S["state_done"], cj)
                X, C = (xt_hi, xt_lo), (c_hi, c_lo)
                if a:
                    pe.wait_ge(S["qk_read"], NPAIR * j + 3)
                for g in range(GATES):
                    if g == 2 and a:
                        pe.wait_ge(S["qk_read"], NPAIR * j + 4)
                    o = ps_proj[g // 2][:, (g % 2) * NT:(g % 2) * NT + NT]
                    for i, (p, q) in enumerate(SPLIT):
                        T.matmul(o, FW[q][:, g, :], X[p][:, :], start=(i == 0), stop=False)
                    for i, (p, q) in enumerate(SPLIT):
                        last = T.matmul(o, FW[q][:, 4 + g, :], C[p][:, :], start=False, stop=(i == 2))
                    if g == 1:
                        last.then_inc(S["gate_ready"], 1)
                for t in range(QT):
                    for i, (p, q) in enumerate(SPLIT):
                        last = T.matmul(ps_proj[1][:, NT + t * D:NT + (t + 1) * D], X[p][:, t * P:(t + 1) * P],
                                        FW[q][:, 3, :], start=(i == 0), stop=(i == 2))
                last.then_inc(S["gate_ready"], 1)

            def body(j, a, b, c):
                bj, cj = j - 1, j - 2
                for s in range(NPAIR):
                    if a:
                        if c and s in (4, 5):
                            pe.wait_ge(S["gate_read"], 2 * cj + s - 3)
                        project(j, s)
                    if b:
                        scores_t(bj, 2 * s)
                        scores_t(bj, 2 * s + 1)
                        if s >= 1:
                            attend(bj, s - 1)
                        if s in (2, 4, 6):
                            sums(bj, s // 2 - 1)
                    if a and s >= 2:
                        scores_for_max(j, 2 * s - 4)
                        scores_for_max(j, 2 * s - 3)
                    if c and s == 1:
                        transpose_xn(cj)
                    if c and s == 3:
                        gates(j, cj, a)
                if b:
                    attend(bj, NPAIR - 1)
                    sums(bj, 3)
                if a:
                    scores_for_max(j, 12)
                    scores_for_max(j, 13)
                    values(j)
                    scores_for_max(j, 14)
                    scores_for_max(j, 15)
                if b:
                    spread(bj)
                if a:
                    transpose_max(j)
                if b:
                    project_out(bj)

            iterations(nc.tensor, body)

            pe.wait_ge(S["state_done"], NB)
            C = (c_hi, c_lo)
            for t in range(QT):
                o = ps_misc[:, t * D:(t + 1) * D]
                for i, (p, q) in enumerate(SPLIT):
                    T.matmul(o, C[p][:, t * P:(t + 1) * P], FW[q][:, 7, :], start=(i == 0), stop=False)
                last = T.matmul(o, bo_one[:, :], bo_sb[:, :], start=False, stop=True)
            last.then_inc(S["cf_ready"], 1)


def constants():
    import numpy as np
    cols, n = const_slices()
    c = np.zeros((P, n), np.float32)

    def put(name, a):
        c[:a.shape[0], cols[name][0]:cols[name][1]] = a

    f = np.arange(0, DH, 2, dtype=np.float32) / np.float32(DH)
    inv = (np.float32(1.0) / np.power(np.float32(10000.0), f)).astype(np.float32)
    ang = np.arange(NT, dtype=np.float32)[:, None] * inv[None, :]
    ang = np.repeat(ang, 2, axis=1).T
    sign = np.where(np.arange(DH) % 2 == 0, -1.0, 1.0).astype(np.float32)[:, None]
    put("cos", np.tile(np.cos(ang), (2, 1)) / np.float32(WS))
    put("sin", np.tile(np.sin(ang) * sign, (2, 1)) / np.float32(WS))
    put("ident", np.eye(P, dtype=np.float32))
    p = np.arange(P)[:, None]
    put("mask_q", np.where(np.arange(SW0)[None, :] > p + NPM, -1e30, 0.0))
    put("mask_k2", np.where((np.arange(NT - Q2)[None, :] < p), -1e30, 0.0))
    sel = np.zeros((P, NPAIR, P))
    shift = np.zeros((P, NH, P))
    for h in range(NH):
        sel[32 * (h % 4) + h // 4, h // 2, 64 * (h % 2):64 * (h % 2) + 64] = 1.0
        shift[[h, 32 + h, 64 + h], h, :] = 1.0
    put("sel_pair", sel.reshape(P, -1))
    put("sel_shift", shift.reshape(P, -1))
    ones = np.zeros((P, 4, 32))
    for g in range(4):
        ones[:, g, g::4] = 1.0
    put("ones_sum", ones.reshape(P, -1))
    return c


def kernel(**inputs):
    import numpy as np
    import concourse.bacc as bacc
    from concourse import mybir as mb
    from concourse.bass_utils import run_bass_kernel_spmd

    a = {k[3:]: np.asarray(v) for k, v in inputs.items()}
    pm = a["attn_persist_mem"]
    ffn = [a["ffn_" + n] for n in ("wf", "wi", "wc", "wo", "uf", "ui", "uc", "uo")]
    arrays = {
        "x": a["attn_x"],
        "w_qkv_t": a["attn_w_qkv"].T,
        "w_out_t": a["attn_w_out"].T,
        "norm_w": a["attn_norm_weight"].reshape(D, 1),
        "pm_k": pm.reshape(NPAIR, 2, NPM, DH).transpose(1, 3, 0, 2).reshape(P, NPAIR * NPM),
        "pm_v": pm.transpose(1, 0, 2).reshape(NPM, DI),
        "ffn_w": np.concatenate([w.T for w in ffn], axis=1),
        "ffn_b": np.stack([a["ffn_" + n] for n in ("bf", "bi", "bc", "in_c")], axis=1),
        "bo_row": a["ffn_bo"].reshape(1, D),
        "consts": constants(),
    }
    arrays = {k: np.ascontiguousarray(v) for k, v in arrays.items()}
    nc = bacc.Bacc("TRN2", target_bir_lowering=False, num_devices=1)
    args = [nc.dram_tensor(k, v.shape, mb.dt.from_np(v.dtype), kind="ExternalInput").ap() for k, v in arrays.items()]
    args.append(nc.dram_tensor("out", (NB, NT, D), mb.dt.float32, kind="ExternalOutput").ap())
    build(nc, *args)
    r = run_bass_kernel_spmd(nc, [arrays], core_ids=[0])
    return r.results[0]["out"]
```

```python
import concourse.bass as bass
from concourse import mybir
from contextlib import ExitStack

NB, NT, D = 32, 256, 128
NH, DH, NPM = 16, 64, 4
DI = NH * DH
P = 128
NPAIR = NH // 2
QT = NT // P
NKEY = NT + NPM
NEND = NKEY - 2 * P
Q1 = P - NPM
QE = NT - NEND
SCOL = NT + (NT - Q1)
CHUNKS = [(0, 0, 0), (1, Q1, NT)]
SW0 = P + NPM
WS = 64.0
RS = 256.0
LOWEST = -3e38
EPS_LN = 1e-5
EPS_RMS = 1.1920928955078125e-07
GATES = 3

CONSTS = [("cos", 2 * NT), ("sin", 2 * NT), ("ident", P), ("mask_q", SW0 + NKEY), ("mask_end", NH * NEND),
          ("sel_pair", NPAIR * P), ("sel_shift", NH), ("sel_shift_end", NH * NEND), ("sel_pm", P),
          ("ones_sum", 4 * 32), ("ones_end", 2 * P)]


def const_slices():
    at, out = 0, {}
    for name, n in CONSTS:
        out[name] = (at, at + n)
        at += n
    return out, at


def wait(eng, sem, count):
    if isinstance(count, int) and count <= 0:
        return
    eng.wait_ge(sem, count)


def build(nc, x, x_last, w_qkv_t, w_out_t, norm_w, pm_k, pm_v, ffn_w, ffn_b, bo_row, consts, out):
    f32, f16, bf16 = mybir.dt.float32, mybir.dt.float16, mybir.dt.bfloat16
    ALU = mybir.AluOpType
    ACT = mybir.ActivationFunctionType
    AX = mybir.AxisListType
    CS, NCONST = const_slices()

    ctx = ExitStack()
    with ctx:
        def sb(name, shape, dt):
            return ctx.enter_context(nc.sbuf_tensor(name, shape, dt))

        def sem(name):
            return ctx.enter_context(nc.semaphore(name))

        x_sb = sb("x_sb", [P, NB, QT * D], f32)
        x_end = sb("x_end", [P, D], f32)
        h_hi = sb("h_hi", [P, NKEY], f16)
        h_lo = sb("h_lo", [P, NKEY], f16)
        h_end = sb("h_end", [P, 2, NB * NEND], f16)
        pre = sb("pre", [P, NB, QT * D], f32)
        pre_f = pre[:, :, :].rearrange("p b n -> p (b n)")
        w_raw = pre_f[:, 0:3 * DI]
        f_raw = pre_f[:, 3 * DI:3 * DI + 8 * P]
        c_raw = pre_f[:, 3 * DI + 8 * P:3 * DI + 8 * P + NCONST]
        assert 3 * DI + 8 * P + NCONST <= NB * QT * D
        w_hi = sb("w_hi", [P, 3 * DI], f16)
        w_lo = sb("w_lo", [P, 3 * DI], f16)
        f_hi = sb("f_hi", [P, 8, P], f16)
        f_lo = sb("f_lo", [P, 8, P], f16)
        wo_sb = sb("wo_sb", [P, NPAIR, D], f32)
        cos = sb("cos", [P, 2 * NT], f32)
        sin = sb("sin", [P, 2 * NT], f32)
        ident_f = sb("ident_f", [P, P], f32)
        ident_b = sb("ident_b", [P, P], bf16)
        mask_q = sb("mask_q", [P, SW0 + NKEY], bf16)
        mask_end = sb("mask_end", [P, NH * NEND], bf16)
        sel_pair = sb("sel_pair", [P, NPAIR, P], f16)
        sel_pm = sb("sel_pm", [96, P], f16)
        pm_parts = sb("pm_parts", [96, DI], f16)
        ones_sum = sb("ones_sum", [P, 4, 32], f32)
        ones_end = sb("ones_end", [P, 2, P], f32)
        bias_raw = sb("bias_raw", [P, 4], f32)
        bias_half = sb("bias_half", [P, 2], f32)
        nw = sb("nw", [P, 1], f32)
        bo_sb = sb("bo_sb", [1, D], f32)
        bo_one = sb("bo_one", [1, P], f32)
        pmk_raw = sb("pmk_raw", [P, NPAIR * NPM], f32)
        sh = sb("sh", [P, QT + 1, 6], f32)
        sh_mv = sb("sh_mv", [P, QT + 1, 2], f32)
        sh_u = sb("sh_u", [P, QT + 1], f32)
        sh_r1 = sb("sh_r1", [P, QT + 1], f32)
        sh_r2 = sb("sh_r2", [P, QT + 1], f32)
        sh_r = sb("sh_r", [P, QT + 1], f32)
        expo = sb("expo", [P, QT + 1], f32)
        gate_col = sb("gate_col", [P, NPAIR], f32)
        eps = sb("eps", [P, QT + 1], f32)
        eps_rms = sb("eps_rms", [P, QT + 1], f32)
        carry = sb("carry", [P, NH + 3], f32)
        xn0 = sb("xn0", [P, (QT + 1) * D], f32)
        rope_a = sb("rope_a", [P, 4, 2 * NT], f32)
        rope_b = sb("rope_b", [P, 2, 2 * NT], f32)
        qk = sb("qk", [P, NH, 2 * NKEY], f32)
        k_end = sb("k_end", [P, 2, NPAIR * NEND], f32)
        qk_h = sb("qk_h", [P, NPAIR, 2 * NKEY], f16)
        v_sb = sb("v_sb", [P, 2, DI], f32)
        v_end = sb("v_end", [NPAIR * NEND, DI], f32)
        top = sb("top", [P, 2, QT, 2, 64], f32)
        masked = sb("masked", [P, SW0 + NKEY], bf16)
        prob = sb("prob", [P, 4, 2, SCOL], f32)
        prob_end = sb("prob_end", [NPAIR * NEND, 2, NPAIR, NEND], f32)
        prob_end_sum = sb("prob_end_sum", [NPAIR * NEND, 2, NEND], f32)
        raw = sb("raw", [P, NPAIR, NT], f32)
        linv = sb("linv", [P, NT], f32)
        linv_hi = sb("linv_hi", [P, NT], f16)
        linv_lo = sb("linv_lo", [P, NT], f16)
        sx = sb("sx", [P, QT, 6], f32)
        sx_mv = sb("sx_mv", [P, QT, 2], f32)
        sx_b = sb("sx_b", [P, QT], f32)
        sx_r = sb("sx_r", [P, QT], f32)
        xn = sb("xn", [P, QT * D], f32)
        xt_hi = sb("xt_hi", [P, NT], f16)
        xt_lo = sb("xt_lo", [P, NT], f16)
        th = sb("th", [P, GATES, NT], f32)
        ga = sb("ga", [P, NT], f32)
        gb = sb("gb", [P, NT], f32)
        c2 = sb("c2", [P, NT], f32)
        c_hi = sb("c_hi", [P, NT], f16)
        c_lo = sb("c_lo", [P, NT], f16)
        cf = sb("cf", [P, QT * D], f32)
        v_end_dram = nc.dram_tensor("v_end_scratch", [P, DI], f32, kind="Internal").ap()

        bank = [ctx.enter_context(nc.psum_tensor(f"bank{i}", [P, 512], f32)) for i in range(8)]
        ps_proj = [bank[0], bank[1]]
        ps_st = [bank[2], bank[3]]
        ps_sm = bank[4]
        ps_pv = bank[5]
        ps_sum = bank[6]
        ps_misc = bank[7]

        S = {n: sem(n) for n in (
            "ld_x0 ld_x1 ld_x2 ld_x3 ld_w ld_c ld_small ld_wo ld_pm ld_end "
            "casts_act casts_dve casts_pool end_tr end_hi end_done ve_ready ve_copied ve_stored "
            "h_stats h_rstd h_xn h_tr h_hi_done h_lo_done "
            "qk_proj qk_read rope_mul rope_sum hi_done qk_done sm_ready max_done top_done top_tr top_copied "
            "st_ready exp_done causal_done pv_ready raw_done sum_ready linv_done r_ready norm_done y_ready x1_done "
            "v_ready v_done v_end sx_done sx_rstd xn_ready xt_ready xt_hi_done xt_lo_done gate_ready gate_read state_done "
            "end_exp end_summed k_end_done cf_ready cf_done fin_sum fin_tanh fin_out stored "
            "dve_pro dve_h dve_b dve_c pool_h pool_b").split()}

        DVE_H, DVE_B, DVE_C, POOL_H = 1, 2, 5, 6
        SHUF = [i ^ 1 for i in range(32)]
        nchunk = 4
        xb = NB // nchunk
        ld_x = [S[f"ld_x{i}"] for i in range(nchunk)]
        x_d = x.rearrange("b (q p) d -> p b q d", p=P)
        out_d = out.rearrange("b (q p) d -> p b q d", p=P)

        def at3(t, b):
            return t[:, b, :] if isinstance(b, int) else t[:, bass.ds(b, 1), :].rearrange("p o n -> p (o n)")

        def at3s(t, b, lo, hi):
            return t[:, b, lo:hi] if isinstance(b, int) else t[:, bass.ds(b, 1), lo:hi].rearrange("p o n -> p (o n)")

        def iterations(eng, body):
            for j in (0, 1, 2):
                body(j, True, True, j >= 1, j >= 2)
            with eng.Fori(3, NB - 1) as j:
                body(j, True, True, True, True)
            body(NB - 1, False, True, True, True)
            body(NB, False, False, True, True)
            body(NB + 1, False, False, False, True)

        OWN = (slice(0, 64), slice(64, 128))

        block = ctx.enter_context(nc.Block())

        @block.sync
        def _(sp):
            sp.dma_start(x_end[:, :], x_last).then_inc(S["ld_end"], 16)
            for i in range(nchunk):
                sp.dma_start(x_sb[:, i * xb:(i + 1) * xb, :].rearrange("p b (q d) -> p b q d", q=QT),
                             x_d[:, i * xb:(i + 1) * xb, :, :]).then_inc(ld_x[i], 16)
            sp.dma_start(v_sb[0:NPM, 0, :], pm_v).then_inc(S["ld_pm"], 16)
            sp.dma_start(wo_sb[:, :, :], w_out_t.rearrange("(c p) d -> p c d", p=P)).then_inc(S["ld_wo"], 16)
            sp.wait_ge(S["ve_copied"], 2)
            sp.dma_start(v_end_dram, raw[:, 0:4, :].rearrange("p c n -> p (c n)")).then_inc(S["ve_stored"], 16)
            sp.wait_ge(S["ve_stored"], 16)

            def body(j, h, a, b, c):
                if not a:
                    return
                wait(sp, S["pv_ready"], NPAIR * j)
                src = v_end_dram[NEND * j:NEND * j + NEND, :] if isinstance(j, int) else v_end_dram[bass.ds(j * NEND, NEND), :]
                for s in range(NPAIR):
                    sp.dma_start(v_end[s * NEND:(s + 1) * NEND, :], src).then_inc(S["v_end"], 16)

            iterations(nc.sync, body)
            for g in range(8):
                sp.wait_ge(S["fin_out"], g + 1)
                sp.dma_start(out_d[:, 4 * g:4 * g + 4, :, :],
                             x_sb[:, 4 * g:4 * g + 4, :].rearrange("p b (q d) -> p b q d", q=QT)).then_inc(S["stored"], 16)
            sp.wait_ge(S["stored"], 16 * 8)

        @block.gpsimd
        def _(pool):
            G = nc.gpsimd
            G.memset(expo[:, :], -0.5).then_inc(S["casts_pool"], 1)
            G.memset(top[:, :, :, :, :], 0.0).then_inc(S["casts_pool"], 1)
            G.memset(pm_parts[:, :], 0.0).then_inc(S["casts_pool"], 1)
            G.memset(h_hi[:, 0:NPM], 0.0).then_inc(S["casts_pool"], 1)
            G.memset(h_lo[:, 0:NPM], 0.0).then_inc(S["casts_pool"], 1)
            G.memset(bo_one[:, :], WS).then_inc(S["casts_pool"], 1)
            G.memset(eps[:, :], EPS_LN).then_inc(S["casts_pool"], 1)
            G.memset(eps_rms[:, :], EPS_RMS).then_inc(S["casts_pool"], 1)

            def factors(n, count, base):
                pool.wait_ge(S["h_stats"], count)
                v = sh_mv[:, 0:n, 1]
                u, r1, r2 = (t[:, 0:n] for t in (sh_u, sh_r1, sh_r2))
                k = [base]

                def link(ins):
                    k[0] = k[0] + 1
                    ins.then_inc(S["pool_h"], 1)
                    pool.wait_ge(S["pool_h"], k[0])

                link(G.tensor_tensor(u, v, eps[:, 0:n], ALU.add))
                link(G.tensor_tensor(r1, u, expo[:, 0:n], ALU.pow))
                link(G.tensor_tensor(u, r1, r1, ALU.mult))
                link(G.tensor_tensor(u, u, v, ALU.mult))
                link(G.tensor_tensor(u, u, eps_rms[:, 0:n], ALU.add))
                link(G.tensor_tensor(r2, u, expo[:, 0:n], ALU.pow))
                G.tensor_tensor(sh_r[:, 0:n], r1, r2, ALU.mult).then_inc(S["h_rstd"], 1)

            pool.wait_ge(S["casts_pool"], 8)
            factors(QT + 1, 1, 0)

            def causal(bj, s):
                pool.wait_ge(S["exp_done"], NH * bj + 2 * s + 2)
                G.tensor_tensor(gate_col[:, s:s + 1], expo[:, 0:1], expo[:, 0:1], ALU.mult)
                c0 = prob[:, s % 4, :, 0:P]
                c1 = prob[:, s % 4, :, NT:NT + P]
                G.affine_select(out=c0, in_=c0, compare_op=ALU.is_ge, fill=0.0, base=NPM,
                                pattern=[[0, 2], [1, P]], channel_multiplier=-1)
                G.affine_select(out=c1, in_=c1, compare_op=ALU.is_ge, fill=0.0, base=0,
                                pattern=[[0, 2], [1, P]], channel_multiplier=-1).then_inc(S["causal_done"], 1)

            def body(j, h, a, b, c):
                bj, cj = j - 1, j - 2
                for s in range(NPAIR):
                    if a:
                        pool.wait_ge(S["qk_read"], NPAIR * j + s + 1)
                        G.tensor_tensor(rope_b[:, s % 2, :], rope_b[:, s % 2, :], sin[:, :], ALU.mult).then_inc(S["rope_mul"], 1)
                    if b and s == NPAIR - 1:
                        causal(bj, s)
                    if a:
                        pool.wait_ge(S["rope_mul"], NPAIR * j + s + 1)
                        G.tensor_tensor(rope_a[:, s % 4, :], rope_a[:, s % 4, :], rope_b[:, s % 2, :],
                                        ALU.add).then_inc(S["rope_sum"], 1)
                    if b and s < NPAIR - 1:
                        causal(bj, s)
                    if h and s == 0:
                        factors(QT, j + 2, POOL_H * (j + 1))
                    if c and s == 2:
                        pool.wait_ge(S["sx_done"], cj + 1)
                        G.tensor_tensor(sx_b[:, :], sx_mv[:, :, 1], eps[:, 0:QT], ALU.add).then_inc(S["pool_b"], 1)
                        pool.wait_ge(S["pool_b"], cj + 1)
                        G.tensor_tensor(sx_r[:, :], sx_b[:, :], expo[:, 0:QT], ALU.pow).then_inc(S["sx_rstd"], 1)

            iterations(nc.gpsimd, body)

        @block.scalar
        def _(act):
            A = nc.scalar
            act.dma_start(w_raw, w_qkv_t).then_inc(S["ld_w"], 16)
            act.dma_start(c_raw, consts).then_inc(S["ld_c"], 16)
            act.dma_start(f_raw, ffn_w).then_inc(S["ld_small"], 16)
            act.dma_start(bias_raw[:, :], ffn_b).then_inc(S["ld_small"], 16)
            act.dma_start(nw[:, :], norm_w).then_inc(S["ld_small"], 16)
            act.dma_start(bo_sb[:, :], bo_row).then_inc(S["ld_small"], 16)
            act.dma_start(pmk_raw[:, :], pm_k).then_inc(S["ld_small"], 16)
            act.wait_ge(S["ld_w"], 16)
            A.activation(w_hi[:, :], w_raw, ACT.Copy, scale=WS).then_inc(S["casts_act"], 1)
            act.wait_ge(S["ld_small"], 80)
            fr = f_raw.rearrange("p (g n) -> p g n", g=8)
            A.activation(f_hi[:, 0:4, :], fr[:, 0:4, :], ACT.Copy, scale=WS).then_inc(S["casts_act"], 1)
            A.activation(f_hi[:, 4:8, :], fr[:, 4:8, :], ACT.Copy, scale=WS / 2).then_inc(S["casts_act"], 1)
            A.activation(bias_half[:, :], bias_raw[:, 0:2], ACT.Copy, scale=0.5).then_inc(S["casts_act"], 1)
            act.wait_ge(S["ld_c"], 16)

            def const(name):
                return c_raw[:, CS[name][0]:CS[name][1]]

            A.copy(cos[:, :], const("cos")).then_inc(S["casts_act"], 1)
            A.copy(sin[:, :], const("sin")).then_inc(S["casts_act"], 1)
            A.copy(ident_f[:, :], const("ident")).then_inc(S["casts_act"], 1)
            A.copy(ident_b[:, :], const("ident")).then_inc(S["casts_act"], 1)
            A.copy(mask_q[:, :], const("mask_q")).then_inc(S["casts_act"], 1)
            A.copy(mask_end[:, :], const("mask_end")).then_inc(S["casts_act"], 1)
            A.copy(sel_pair[:, :, :].rearrange("p c n -> p (c n)"), const("sel_pair")).then_inc(S["casts_act"], 1)
            A.copy(sel_pm[:, :], const("sel_pm")[0:96, :]).then_inc(S["casts_act"], 1)
            A.copy(k_end[:, :, :].rearrange("p e n -> p (e n)"), const("sel_shift_end")).then_inc(S["casts_act"], 1)
            A.copy(ones_end[:, :, :].rearrange("p e n -> p (e n)"), const("ones_end")).then_inc(S["casts_act"], 1)
            A.copy(qk[:, :, NT:NT + NKEY], const("sel_shift").unsqueeze(2).to_broadcast([P, NH, NKEY])).then_inc(S["casts_act"], 1)
            A.copy(ones_sum[:, :, :].rearrange("p c n -> p (c n)"), const("ones_sum")).then_inc(S["casts_act"], 1)

            def h_high(count, read=0):
                act.wait_ge(S["h_tr"], count)
                wait(act, S["v_ready"], read)
                A.activation(h_hi[:, NPM:NKEY], ps_st[0][:, 0:NT], ACT.Copy, scale=nw[:, :]).then_inc(S["h_hi_done"], 1)

            act.wait_ge(S["end_tr"], 1)
            A.activation(h_end[:, 0, :], ps_sum[:, 0:P], ACT.Copy, scale=nw[:, :]).then_inc(S["end_hi"], 1)
            h_high(1)
            for u in range(2):
                act.wait_ge(S["ve_ready"], u + 1)
                A.activation(raw[:, 2 * u:2 * u + 2, :].rearrange("p c n -> p (c n)"), bank[6 + u][:, :], ACT.Copy,
                             scale=1.0 / WS).then_inc(S["ve_copied"], 1)

            def hi(j, s):
                act.wait_ge(S["rope_sum"], NPAIR * j + s + 1)
                wait(act, S["sm_ready"], NH * (j - 1) + 2 * s + 2)
                A.activation(qk_h[:, s, :].rearrange("p (u n) -> p u n", u=2)[:, :, 0:NT],
                             rope_a[:, s % 4, :].rearrange("p (u n) -> p u n", u=2), ACT.Copy).then_inc(S["hi_done"], 1)

            def full(j, s):
                wait(act, S["st_ready"], NH * (j - 1) + 2 * s + 2)
                if isinstance(j, int) and j == 0 and s == 0:
                    act.wait_ge(S["casts_dve"], 5)
                for e in range(2):
                    h, own = 2 * s + e, OWN[e]
                    ins = A.activation(qk[own, h, 0:2 * (NT + NPM)].rearrange("p (u n) -> p u n", u=2)[:, :, 0:NT],
                                       rope_a[own, s % 4, :].rearrange("p (u n) -> p u n", u=2), ACT.Copy)
                ins.then_inc(S["qk_done"], 1)

            def exp(bj, h):
                s = h // 2
                act.wait_ge(S["st_ready"], NH * bj + h + 1)
                if h % 2 == 0:
                    wait(act, S["sum_ready"], 4 * bj + (s - 4) // 2 + 1)
                if h == 2:
                    wait(act, S["pv_ready"], NPAIR * bj)
                    wait(act, S["end_summed"], bj)
                    A.activation(prob_end[:, :, :, :].rearrange("p e s q -> p (e s q)"),
                                 ps_st[0][0:NPAIR * NEND, SCOL:SCOL + NH * NEND], ACT.Exp).then_inc(S["end_exp"], 1)
                A.activation(prob[:, s % 4, h % 2, :], ps_st[h % 2][:, 0:SCOL], ACT.Exp).then_inc(S["exp_done"], 1)

            def spread_top(j, half):
                act.wait_ge(S["top_tr"], 2 * j + half + 1)
                wait(act, S["st_ready"], NH * (j - 1) + NH // 2 * (half + 1))
                o = (ps_misc, ps_sm)[half]
                for e in range(2):
                    h0, h1 = NH // 2 * half + e, NH // 2 * (half + 1)
                    ins = A.activation(qk[OWN[1 - e], h0:h1:2, 0:NT],
                                       o[OWN[1 - e], 0:NT].unsqueeze(1).to_broadcast([64, NPAIR // 2, NT]), ACT.Copy)
                ins.then_inc(S["top_copied"], 1)

            def raw_copy(bj, s):
                act.wait_ge(S["pv_ready"], NPAIR * bj + s + 1)
                if s == 0:
                    wait(act, S["y_ready"], bj)
                if isinstance(bj, int) and bj == 0 and s == 0:
                    act.wait_ge(S["ve_stored"], 16)
                A.activation(raw[:, s, :], ps_pv[:, 0:NT], ACT.Copy, scale=1.0 / RS).then_inc(S["raw_done"], 1)

            def body(j, h, a, b, c):
                bj, cj = j - 1, j - 2
                for s in range(NPAIR):
                    if b:
                        exp(bj, 2 * s)
                        exp(bj, 2 * s + 1)
                    if c and s == 4:
                        act.wait_ge(S["xt_ready"], cj + 1)
                        wait(act, S["gate_ready"], 2 * cj)
                        A.activation(xt_hi[:, :], ps_misc[:, 0:NT], ACT.Copy).then_inc(S["xt_hi_done"], 1)
                    if a and s >= 1:
                        hi(j, s - 1)
                        full(j, s - 1)
                    if c and s == 5:
                        act.wait_ge(S["gate_ready"], 2 * cj + 1)
                        wait(act, S["state_done"], cj)
                        A.activation(th[:, 0, :], ps_misc[:, 0:NT], ACT.Tanh, bias=bias_half[:, 0:1],
                                     scale=0.5 / WS)
                        A.activation(th[:, 1, :], ps_misc[:, NT:2 * NT], ACT.Tanh, bias=bias_half[:, 1:2],
                                     scale=0.5 / WS).then_inc(S["gate_read"], 1)
                        act.wait_ge(S["gate_ready"], 2 * cj + 2)
                        A.activation(th[:, 2, :], ps_proj[0][:, 0:NT], ACT.Tanh, bias=bias_raw[:, 2:3],
                                     scale=1.0 / WS)
                        A.activation(at3(pre, cj), ps_proj[0][:, NT:2 * NT], ACT.Copy).then_inc(S["gate_read"], 1)
                    if b and s >= 1:
                        raw_copy(bj, s - 1)
                    if a and s == 6:
                        spread_top(j, 0)
                if a:
                    def value_copy(n):
                        act.wait_ge(S["v_ready"], 4 * j + n + 1)
                        if n == 0:
                            wait(act, S["pv_ready"], NPAIR * j)
                        A.activation(v_sb[:, n // 2, (n % 2) * 512:(n % 2) * 512 + 512], ps_proj[n % 2][:, :], ACT.Copy,
                                     scale=1.0 / WS).then_inc(S["v_done"], 1)
                    hi(j, NPAIR - 1)
                    value_copy(0)
                if b:
                    raw_copy(bj, NPAIR - 1)
                if a:
                    for n in range(1, 4):
                        value_copy(n)
                if h:
                    h_high(j + 2, 4 * j + 4)
                if a:
                    full(j, NPAIR - 1)
                    act.wait_ge(S["qk_done"], NPAIR * j + NPAIR)
                    wait(act, S["st_ready"], NH * (j - 1) + 3)
                    for e in range(2):
                        ins = A.activation(k_end[OWN[e], e, :].rearrange("p (s n) -> p s n", s=NPAIR),
                                           qk[OWN[e], e::2, NKEY + QE:NKEY + NT], ACT.Copy)
                    ins.then_inc(S["k_end_done"], 1)
                    spread_top(j, 1)

            iterations(nc.scalar, body)

            act.wait_ge(S["cf_ready"], 1)
            A.copy(cf[:, :], ps_misc[:, 0:NT]).then_inc(S["cf_done"], 1)
            for g in range(8):
                act.wait_ge(S["fin_sum"], g + 1)
                v = pre[:, 4 * g:4 * g + 4, :]
                A.activation(v, v, ACT.Tanh, scale=1.0 / WS).then_inc(S["fin_tanh"], 1)

        @block.vector
        def _(dve):
            V = nc.vector
            chain = [0]

            def link(ins):
                chain[0] += 1
                ins.then_inc(S["dve_pro"], 1)
                dve.wait_ge(S["dve_pro"], chain[0])

            dve.wait_ge(S["casts_act"], 1)
            V.scalar_tensor_tensor(w_lo[:, :], w_raw, WS, w_hi[:, :], ALU.mult, ALU.subtract).then_inc(S["casts_dve"], 1)
            dve.wait_ge(S["casts_act"], 3)
            fr = f_raw.rearrange("p (g n) -> p g n", g=8)
            V.scalar_tensor_tensor(f_lo[:, 0:4, :], fr[:, 0:4, :], WS, f_hi[:, 0:4, :], ALU.mult,
                                   ALU.subtract).then_inc(S["casts_dve"], 1)
            V.scalar_tensor_tensor(f_lo[:, 4:8, :], fr[:, 4:8, :], WS / 2, f_hi[:, 4:8, :], ALU.mult,
                                   ALU.subtract).then_inc(S["casts_dve"], 1)
            dve.wait_ge(S["casts_pool"], 3)
            dve.wait_ge(S["casts_act"], 16)
            pk = pmk_raw[:, :].rearrange("p (c n) -> p c n", c=NPAIR)
            for e in range(2):
                link(V.tensor_copy(qk[OWN[e], e::2, NT:NT + NPM], pk[OWN[e], :, :]))
            link(V.tensor_copy(qk_h[:, :, NT:NT + NPM], pk))
            V.memset(ga[:, :], 0.0).then_inc(S["casts_dve"], 1)
            dve.wait_ge(S["ld_pm"], 16)
            t = v_sb[0:NPM, 0, :]
            link(V.tensor_scalar(t, t, WS, None, ALU.mult))
            link(V.tensor_copy(pm_parts[0:NPM, :], t))
            link(V.tensor_tensor(t, t, pm_parts[0:NPM, :], ALU.subtract))
            link(V.tensor_copy(pm_parts[32:32 + NPM, :], t))
            link(V.tensor_copy(v_sb[32:32 + NPM, 0, :], t))
            t = v_sb[32:32 + NPM, 0, :]
            link(V.tensor_tensor(t, t, pm_parts[32:32 + NPM, :], ALU.subtract))
            V.tensor_copy(pm_parts[64:64 + NPM, :], t).then_inc(S["casts_dve"], 1)
            link(V.memset(c2[:, :], 2.0))
            link(V.tensor_scalar(c2[:, :], c2[:, :], bias_raw[:, 3:4], None, ALU.mult))
            link(V.tensor_copy(c_hi[:, :], c2[:, :]))
            link(V.tensor_tensor(c_lo[:, :], c2[:, :], c_hi[:, :], ALU.subtract))

            def moments(src, mv, n):
                for q in range(n):
                    last = V.bn_aggr(mv[:, q, :], src[:, q, :])
                return last

            def normalise(q, src):
                return V.tensor_scalar(xn0[:, q * D:(q + 1) * D], src, sh_mv[:, q, 0:1], sh_r[:, q:q + 1],
                                       ALU.subtract, ALU.mult)

            def h_low(count):
                dve.wait_ge(S["h_hi_done"], count)
                V.scalar_tensor_tensor(h_lo[:, NPM:NKEY], ps_st[0][:, 0:NT], nw[:, :], h_hi[:, NPM:NKEY],
                                       ALU.mult, ALU.subtract).then_inc(S["h_lo_done"], 1)

            dve.wait_ge(S["ld_end"], 16)
            V.bn_stats(sh[:, QT, :], x_end[:, :])
            dve.wait_ge(ld_x[0], 16)
            V.bn_stats(sh[:, 0, :], x_sb[:, 0, 0:D])
            link(V.bn_stats(sh[:, 1, :], x_sb[:, 0, D:2 * D]))
            moments(sh, sh_mv, QT + 1).then_inc(S["h_stats"], 1)
            dve.wait_ge(S["h_rstd"], 1)
            normalise(QT, x_end[:, :])
            for q in range(QT):
                last = normalise(q, x_sb[:, 0, q * D:(q + 1) * D])
            last.then_inc(S["h_xn"], 1)
            dve.wait_ge(S["end_hi"], 1)
            V.scalar_tensor_tensor(h_end[:, 1, :], ps_sum[:, 0:P], nw[:, :], h_end[:, 0, :],
                                   ALU.mult, ALU.subtract).then_inc(S["end_done"], 1)
            h_low(1)
            for i in range(1, nchunk):
                dve.wait_ge(ld_x[i], 16)

            def body(j, h, a, b, c):
                bj, cj = j - 1, j - 2
                kh, kb, kc = [0], [0], [0]

                def carry_wait(column):
                    V.tensor_tensor(carry[:, column:column + 1], expo[:, 0:1], expo[:, 0:1], ALU.mult)

                def link_h(ins):
                    kh[0] += 1
                    ins.then_inc(S["dve_h"], 1)
                    dve.wait_ge(S["dve_h"], DVE_H * j + kh[0])

                def link_b(ins):
                    kb[0] += 1
                    ins.then_inc(S["dve_b"], 1)
                    dve.wait_ge(S["dve_b"], DVE_B * bj + kb[0])

                def link_c(ins):
                    kc[0] += 1
                    ins.then_inc(S["dve_c"], 1)
                    dve.wait_ge(S["dve_c"], DVE_C * cj + kc[0])

                def maxima(h):
                    dve.wait_ge(S["sm_ready"], NH * j + h + 1)
                    if h in (0, NH // 2):
                        wait(dve, S["top_tr"], 2 * (j - 1) + 1 + h // (NH // 2))
                        if isinstance(j, int) and j == 0:
                            dve.wait_ge(S["casts_pool"], 2)
                    carry_wait(h)
                    for q, c0, n in ((0, 0, SW0), (1, SW0, NKEY)):
                        ins = V.tensor_tensor_reduce(masked[:, c0:c0 + n], ps_sm[:, c0:c0 + n], mask_q[:, c0:c0 + n], 1.0,
                                                     LOWEST, ALU.add, ALU.max, top[:, h // 8, q, 0, h:h + 1])
                    ins.then_inc(S["max_done"], 1)

                def copy_top(half):
                    n = NH // 2
                    dve.wait_ge(S["max_done"], NH * j + n * (half + 1))
                    V.tensor_copy(top[:, half, :, 1, n * half:n * half + n],
                                  top[:, half, :, 0, n * half:n * half + n]).then_inc(S["top_done"], 1)

                def divide(n):
                    dve.wait_ge(S["r_ready"], 4 * cj + n + 1)
                    if n == 0:
                        dve.wait_ge(S["raw_done"], NPAIR * cj + NPAIR)
                    r = (ps_pv, ps_sum)[n % 2]
                    o = raw[:, 2 * n:2 * n + 2, :].rearrange("p c n -> p (c n)")
                    V.tensor_tensor(o, r[:, :], o, ALU.mult).then_inc(S["norm_done"], 1)

                for s in range(NPAIR):
                    if a:
                        if s >= 2:
                            maxima(2 * s - 4)
                        dve.wait_ge(S["qk_proj"], NPAIR * j + s + 1)
                        wait(dve, S["qk_done"], NPAIR * j + s - 3)
                        wait(dve, S["rope_sum"], NPAIR * j + s - 1)
                        V.tensor_tensor(rope_a[:, s % 4, :], ps_proj[s % 2][:, :], cos[:, :], ALU.mult)
                        V.stream_shuffle(rope_b[:, s % 2, :], ps_proj[s % 2][:, :], SHUF).then_inc(S["qk_read"], 1)
                    if b and s == 2:
                        dve.wait_ge(S["end_exp"], bj + 1)
                        wait(dve, S["sum_ready"], 4 * bj)
                        V.tensor_reduce(prob_end_sum[:, :, :], prob_end[:, :, :, :].rearrange("p e s q -> p e q s"), AX.X,
                                        ALU.add).then_inc(S["end_summed"], 1)
                    if c and s <= 1:
                        divide(2 * s)
                        divide(2 * s + 1)
                    if a and s >= 2:
                        maxima(2 * s - 3)
                    if c and s == 3:
                        dve.wait_ge(S["sx_rstd"], cj + 1)
                        wait(dve, S["xt_ready"], cj)
                        for q in range(QT):
                            last = V.tensor_scalar(xn[:, q * D:(q + 1) * D], at3s(x_sb, cj, q * D, (q + 1) * D),
                                                   sx_mv[:, q, 0:1], sx_r[:, q:q + 1], ALU.subtract, ALU.mult)
                        last.then_inc(S["xn_ready"], 1)
                    if a and s == 5:
                        copy_top(0)
                    if h and s == 0:
                        dve.wait_ge(S["h_xn"], j + 1)
                        V.bn_stats(sh[:, 0, :], at3s(x_sb, j + 1, 0, D))
                        link_h(V.bn_stats(sh[:, 1, :], at3s(x_sb, j + 1, D, 2 * D)))
                        carry_wait(NH + 2)
                        moments(sh, sh_mv, QT).then_inc(S["h_stats"], 1)
                    if c and s == 1:
                        dve.wait_ge(S["y_ready"], cj + 1)
                        V.tensor_tensor(at3(x_sb, cj), ps_misc[:, 0:QT * D], at3(x_sb, cj), ALU.add).then_inc(S["x1_done"], 1)
                        dve.wait_ge(S["x1_done"], cj + 1)
                        carry_wait(NH)
                        V.bn_stats(sx[:, 0, :], at3s(x_sb, cj, 0, D))
                        link_c(V.bn_stats(sx[:, 1, :], at3s(x_sb, cj, D, 2 * D)))
                        carry_wait(NH + 1)
                        moments(sx, sx_mv, QT).then_inc(S["sx_done"], 1)
                    if h and s == 5:
                        dve.wait_ge(S["h_rstd"], j + 2)
                        dve.wait_ge(S["h_tr"], j + 1)
                        for q in range(QT):
                            last = normalise(q, at3s(x_sb, j + 1, q * D, (q + 1) * D))
                        last.then_inc(S["h_xn"], 1)
                    if c and s == 4:
                        dve.wait_ge(S["xt_hi_done"], cj + 1)
                        V.tensor_tensor(xt_lo[:, :], ps_misc[:, 0:NT], xt_hi[:, :], ALU.subtract).then_inc(S["xt_lo_done"], 1)
                    if c and s == 6:
                        dve.wait_ge(S["gate_read"], 2 * cj + 2)
                        link_c(V.scalar_tensor_tensor(ga[:, :], th[:, 0, :], 1.0, c2[:, :], ALU.add, ALU.mult))
                        link_c(V.scalar_tensor_tensor(gb[:, :], th[:, 1, :], 1.0, th[:, 2, :], ALU.add, ALU.mult))
                        link_c(V.scalar_tensor_tensor(c2[:, :], ga[:, :], 0.5, gb[:, :], ALU.mult, ALU.add))
                        link_c(V.tensor_copy(c_hi[:, :], c2[:, :]))
                        V.tensor_tensor(c_lo[:, :], c2[:, :], c_hi[:, :], ALU.subtract).then_inc(S["state_done"], 1)
                if a:
                    for n in range(12, NH):
                        maxima(n)
                    copy_top(1)
                if h:
                    h_low(j + 2)
                if b:
                    dve.wait_ge(S["sum_ready"], 4 * bj + 4)
                    link_b(V.reciprocal(linv[:, :], ps_sum[:, 0:NT]))
                    link_b(V.tensor_copy(linv_hi[:, :], linv[:, :]))
                    V.tensor_tensor(linv_lo[:, :], linv[:, :], linv_hi[:, :], ALU.subtract).then_inc(S["linv_done"], 1)
                assert not h or kh[0] == DVE_H
                assert not b or kb[0] == DVE_B
                assert not c or kc[0] == DVE_C

            iterations(nc.vector, body)

            dve.wait_ge(S["cf_done"], 1)

            def fin_add(g):
                v = pre[:, 4 * g:4 * g + 4, :]
                V.tensor_tensor(v, v, cf[:, :].unsqueeze(1).to_broadcast([P, 4, QT * D]), ALU.add).then_inc(S["fin_sum"], 1)

            def fin_res(g):
                dve.wait_ge(S["fin_tanh"], g + 1)
                v = pre[:, 4 * g:4 * g + 4, :]
                o = x_sb[:, 4 * g:4 * g + 4, :]
                V.tensor_tensor(o, o, v, ALU.add).then_inc(S["fin_out"], 1)

            fin_add(0)
            for g in range(1, 8):
                fin_add(g)
                fin_res(g - 1)
            fin_res(7)

        @block.tensor
        def _(pe):
            T = nc.tensor
            pe.wait_ge(S["casts_act"], 16)
            def transpose_x(j):
                pe.wait_ge(S["h_xn"], j + 1)
                for q in range(QT):
                    last = T.transpose(ps_st[0][:, q * P:(q + 1) * P], xn0[:, q * D:(q + 1) * D], ident_f[:, :])
                last.then_inc(S["h_tr"], 1)

            pe.wait_ge(S["h_xn"], 1)
            T.transpose(ps_sum[:, 0:P], xn0[:, QT * D:(QT + 1) * D], ident_f[:, :]).then_inc(S["end_tr"], 1)
            transpose_x(0)
            pe.wait_ge(S["end_done"], 1)
            pe.wait_ge(S["casts_dve"], 5)
            pe.wait_ge(S["casts_pool"], 6)
            SPLIT = [(0, 0), (0, 1), (1, 0)]
            H, W, FW = (h_hi, h_lo), (w_hi, w_lo), (f_hi, f_lo)
            for u in range(2):
                for i, (p, q) in enumerate(SPLIT):
                    last = T.matmul(bank[6 + u][:, :], h_end[:, p, :], W[q][:, 2 * DI + u * 512:2 * DI + u * 512 + 512],
                                    start=(i == 0), stop=(i == 2))
                last.then_inc(S["ve_ready"], 1)
            pe.wait_ge(S["ve_copied"], 2)
            pe.wait_ge(S["ld_wo"], 16)

            def project(j, s):
                if s == 0:
                    pe.wait_ge(S["h_lo_done"], j + 1)
                if s >= 2:
                    pe.wait_ge(S["qk_read"], NPAIR * j + s - 1)
                else:
                    wait(pe, S["v_done"], 4 * j - 1 + s)
                for u in range(2):
                    col = u * DI + s * P
                    for i, (p, q) in enumerate(SPLIT):
                        last = T.matmul(ps_proj[s % 2][:, u * NT:(u + 1) * NT], W[q][:, col:col + P],
                                        H[p][:, NPM:NKEY], start=(i == 0), stop=(i == 2))
                last.then_inc(S["qk_proj"], 1)

            def values(j, n):
                if n < 2:
                    pe.wait_ge(S["qk_read"], NPAIR * j + 7 + n)
                else:
                    pe.wait_ge(S["v_done"], 4 * j + n - 1)
                kc, col = n // 2, 2 * DI + (n % 2) * 512
                for i, (p, q) in enumerate(SPLIT):
                    last = T.matmul(ps_proj[n % 2][:, :], H[p][:, kc * P:kc * P + P], W[q][:, col:col + 512],
                                    start=(i == 0), stop=(i == 2 and kc == 1))
                if kc == 0:
                    last = T.matmul(ps_proj[n % 2][:, :], sel_pm[:, :], pm_parts[:, (n % 2) * 512:(n % 2) * 512 + 512],
                                    start=False, stop=True)
                last.then_inc(S["v_ready"], 1)

            def scores_for_max(j, h):
                s, e = h // 2, h % 2
                if e == 0:
                    pe.wait_ge(S["hi_done"], NPAIR * j + s + 1)
                wait(pe, S["max_done"], NH * j + h)
                if h == 0:
                    wait(pe, S["top_copied"], 2 * j)
                for q, c0, n in ((0, 0, SW0), (1, SW0, NKEY)):
                    last = T.matmul(ps_sm[:, c0:c0 + n], qk_h[OWN[e], s, q * P:(q + 1) * P], qk_h[OWN[e], s, NT:NT + n],
                                    start=True, stop=True)
                last.then_inc(S["sm_ready"], 1)

            def transpose_top(j, half):
                pe.wait_ge(S["top_done"], 2 * j + half + 1)
                if half == 0:
                    wait(pe, S["gate_read"], 2 * (j - 2) + 1)
                o = (ps_misc, ps_sm)[half]
                for q in range(QT):
                    last = T.transpose(o[:, q * P:(q + 1) * P], top[:, half, q, :, :].rearrange("p a b -> p (a b)"),
                                       ident_f[:, :])
                last.then_inc(S["top_tr"], 1)

            def scores_t(bj, h):
                s, e = h // 2, h % 2
                if h == 0:
                    pe.wait_ge(S["top_copied"], 2 * bj + 1)
                if h == 2:
                    pe.wait_ge(S["top_copied"], 2 * bj + 2)
                if e == 0:
                    pe.wait_ge(S["qk_done"], NPAIR * bj + s + 1)
                wait(pe, S["exp_done"], NH * bj + h - 1)
                ps = ps_st[e]
                for kc, q0, c0 in CHUNKS:
                    last = T.matmul(ps[:, c0:c0 + NT - q0], qk[:, h, NT + kc * P:NT + (kc + 1) * P], qk[:, h, q0:NT],
                                    start=True, stop=True)
                if h == 2:
                    pe.wait_ge(S["k_end_done"], bj + 1)
                    n = NPAIR * NEND
                    for e in range(2):
                        o = ps[0:n, SCOL + e * n:SCOL + (e + 1) * n]
                        T.matmul(o, k_end[:, e, :], qk[:, e::2, QE:NT], start=True, stop=False)
                        last = T.matmul(o, ident_b[:, 0:n], mask_end[:, e * n:(e + 1) * n], start=False, stop=True)
                last.then_inc(S["st_ready"], 1)

            def attend(bj, s):
                pe.wait_ge(S["causal_done"], NPAIR * bj + s + 1)
                wait(pe, S["raw_done"], NPAIR * bj + s)
                if s == 0:
                    pe.wait_ge(S["v_done"], 4 * bj + 4)
                    pe.wait_ge(S["v_end"], 16 * NPAIR * (bj + 1))
                    pe.wait_ge(S["end_exp"], bj + 1)
                    wait(pe, S["norm_done"], 4 * bj)
                for kc, q0, c0 in CHUNKS:
                    for e in range(2):
                        col = (2 * s + e) * DH
                        T.matmul(ps_pv[64 * e:64 * e + 64, q0:NT], v_sb[:, kc, col:col + DH],
                                 prob[:, s % 4, e, c0:c0 + NT - q0], start=(kc == 0), stop=False)
                for e in range(2):
                    col = (2 * s + e) * DH
                    last = T.matmul(ps_pv[64 * e:64 * e + 64, QE:NT], v_end[:, col:col + DH], prob_end[:, e, s, :],
                                    start=False, stop=True)
                last.then_inc(S["pv_ready"], 1)

            def sums(bj, g):
                for kc, q0, c0 in CHUNKS:
                    for r in range(4):
                        last = T.matmul(ps_sum[32 * r:32 * r + 32, q0:NT], ones_sum[:, g, :],
                                        prob[:, (2 * g + r // 2) % 4, r % 2, c0:c0 + NT - q0],
                                        start=(g == 0 and kc == 0), stop=False, skip_group_check=True)
                if g == 3:
                    pe.wait_ge(S["end_summed"], bj + 1)
                    for e in range(2):
                        last = T.matmul(ps_sum[:, QE:NT], ones_end[0:NPAIR * NEND, e, :], prob_end_sum[:, e, :],
                                        start=False, stop=(e == 1), skip_group_check=True)
                last.then_inc(S["sum_ready"], 1)

            def spread(bj, n):
                if n == 0:
                    pe.wait_ge(S["linv_done"], bj + 1)
                    pe.wait_ge(S["raw_done"], NPAIR * bj + NPAIR)
                if n >= 2:
                    pe.wait_ge(S["norm_done"], 4 * bj + n - 1)
                r = (ps_pv, ps_sum)[n % 2]
                for u in range(2):
                    T.matmul(r[:, u * NT:(u + 1) * NT], sel_pair[:, 2 * n + u, :], linv_hi[:, :], start=True, stop=False)
                    last = T.matmul(r[:, u * NT:(u + 1) * NT], sel_pair[:, 2 * n + u, :], linv_lo[:, :],
                                    start=False, stop=True)
                last.then_inc(S["r_ready"], 1)

            def project_out(bj, n, b):
                pe.wait_ge(S["norm_done"], 4 * bj + n + 1)
                if n == 0 and b:
                    pe.wait_ge(S["top_copied"], 2 * (bj + 1) + 1)
                for s in (2 * n, 2 * n + 1):
                    for q in range(QT):
                        last = T.matmul(ps_misc[:, q * D:(q + 1) * D], raw[:, s, q * P:(q + 1) * P], wo_sb[:, s, :],
                                        start=(s == 0 and q == 0), stop=(s == NPAIR - 1 and q == QT - 1),
                                        skip_group_check=True)
                if n == 3:
                    last.then_inc(S["y_ready"], 1)

            def transpose_xn(cj):
                pe.wait_ge(S["xn_ready"], cj + 1)
                for q in range(QT):
                    last = T.transpose(ps_misc[:, q * P:(q + 1) * P], xn[:, q * D:(q + 1) * D], ident_f[:, :])
                last.then_inc(S["xt_ready"], 1)

            def gates(j, cj, a):
                pe.wait_ge(S["xt_lo_done"], cj + 1)
                wait(pe, S["state_done"], cj)
                X, C = (xt_hi, xt_lo), (c_hi, c_lo)
                if a:
                    pe.wait_ge(S["qk_read"], NPAIR * j + 5)
                for g in range(GATES):
                    o = (ps_misc, ps_proj[0])[g // 2][:, (g % 2) * NT:(g % 2) * NT + NT]
                    for i, (p, q) in enumerate(SPLIT):
                        T.matmul(o, FW[q][:, g, :], X[p][:, :], start=(i == 0), stop=False)
                    for i, (p, q) in enumerate(SPLIT):
                        last = T.matmul(o, FW[q][:, 4 + g, :], C[p][:, :], start=False, stop=(i == 2))
                    if g == 1:
                        last.then_inc(S["gate_ready"], 1)
                for t in range(QT):
                    for i, (p, q) in enumerate(SPLIT):
                        last = T.matmul(ps_proj[0][:, NT + t * D:NT + (t + 1) * D], X[p][:, t * P:(t + 1) * P],
                                        FW[q][:, 3, :], start=(i == 0), stop=(i == 2))
                last.then_inc(S["gate_ready"], 1)

            def body(j, h, a, b, c):
                bj, cj = j - 1, j - 2
                for s in range(NPAIR):
                    if a:
                        if c and s == 6:
                            pe.wait_ge(S["gate_read"], 2 * cj + 2)
                        if s >= 2:
                            scores_for_max(j, 2 * s - 4)
                        project(j, s)
                    if c and s == 1:
                        project_out(cj, 1, b)
                        spread(cj, 3)
                    if b:
                        scores_t(bj, 2 * s)
                    if a and s >= 2:
                        scores_for_max(j, 2 * s - 3)
                    if b:
                        scores_t(bj, 2 * s + 1)
                    if a and s == 6:
                        transpose_top(j, 0)
                    if c and s == 0:
                        spread(cj, 0)
                        spread(cj, 1)
                        project_out(cj, 0, b)
                        spread(cj, 2)
                    if c and s == 1:
                        project_out(cj, 2, b)
                        project_out(cj, 3, b)
                    if c and s == 5:
                        gates(j, cj, a)
                    if b and s >= 1:
                        attend(bj, s - 1)
                        if s in (2, 4, 6):
                            sums(bj, s // 2 - 1)
                    if c and s == 3:
                        transpose_xn(cj)
                for n in range(4):
                    if a:
                        scores_for_max(j, 12 + n)
                        values(j, n)
                    if b and n == 0:
                        attend(bj, NPAIR - 1)
                if h:
                    wait(pe, S["exp_done"], NH * bj + NH - 1)
                    transpose_x(j + 1)
                if b:
                    sums(bj, 3)
                if a:
                    transpose_top(j, 1)

            iterations(nc.tensor, body)

            pe.wait_ge(S["state_done"], NB)
            C = (c_hi, c_lo)
            for t in range(QT):
                o = ps_misc[:, t * D:(t + 1) * D]
                for i, (p, q) in enumerate(SPLIT):
                    T.matmul(o, C[p][:, t * P:(t + 1) * P], FW[q][:, 7, :], start=(i == 0), stop=False)
                last = T.matmul(o, bo_one[:, :], bo_sb[:, :], start=False, stop=True)
            last.then_inc(S["cf_ready"], 1)


def constants():
    import numpy as np
    cols, n = const_slices()
    c = np.zeros((P, n), np.float32)

    def put(name, a):
        c[:a.shape[0], cols[name][0]:cols[name][1]] = a

    f = np.arange(0, DH, 2, dtype=np.float32) / np.float32(DH)
    inv = (np.float32(1.0) / np.power(np.float32(10000.0), f)).astype(np.float32)
    ang = np.arange(NT, dtype=np.float32)[:, None] * inv[None, :]
    ang = np.repeat(ang, 2, axis=1).T
    sign = np.where(np.arange(DH) % 2 == 0, -1.0, 1.0).astype(np.float32)[:, None]
    both = np.array([DH ** -0.5, 1.0], np.float32) / np.float32(WS)
    put("cos", np.concatenate([np.tile(np.cos(ang), (2, 1)) * f for f in both], axis=1))
    put("sin", np.concatenate([np.tile(np.sin(ang) * sign, (2, 1)) * f for f in both], axis=1))
    put("ident", np.eye(P, dtype=np.float32))
    p = np.arange(P)[:, None]
    mask = np.zeros((P, SW0 + NKEY))
    mask[:, 0:SW0] = np.where(np.arange(SW0)[None, :] > p + NPM, -1e30, 0.0)
    mask[:, SW0 + P:] = mask[:, 0:SW0]
    put("mask_q", mask)
    n = NPAIR * NEND
    row, col = np.arange(n)[:, None], np.arange(n)[None, :]
    own = (row // NEND == col // NEND) & (row % NEND <= col % NEND)
    put("mask_end", np.tile(np.where(own, 0.0, -1e30), (1, 2)))
    sel = np.zeros((P, NPAIR, P))
    shift, shift_end, ones_end = np.zeros((P, NH)), np.zeros((P, 2, n)), np.zeros((P, 2, P))
    sel_pm = np.zeros((P, P))
    for h in range(NH):
        sel[32 * (h % 4) + h // 4, h // 2, 64 * (h % 2):64 * (h % 2) + 64] = 1.0
        s, e = h // 2, h % 2
        shift[64 * (1 - e) + h, h] = -1.0
        shift_end[64 * (1 - e) + h, e, s * NEND:(s + 1) * NEND] = -1.0
        ones_end[s * NEND:(s + 1) * NEND, e, 32 * (h % 4) + h // 4:32 * (h % 4) + 32:4] = 1.0 / RS
    for part in range(3):
        sel_pm[32 * part + np.arange(NPM), np.arange(NPM)] = 1.0
    put("sel_pair", sel.reshape(P, -1))
    put("sel_shift", shift)
    put("sel_shift_end", shift_end.reshape(P, -1))
    put("ones_end", ones_end.reshape(P, -1))
    put("sel_pm", sel_pm)
    ones = np.zeros((P, 4, 32))
    for g in range(4):
        ones[:, g, g::4] = 1.0 / RS
    put("ones_sum", ones.reshape(P, -1))
    return c


def kernel(**inputs):
    import numpy as np
    import concourse.bacc as bacc
    from concourse import mybir as mb
    from concourse.bass_utils import run_bass_kernel_spmd

    a = {k[3:]: np.asarray(v) for k, v in inputs.items()}
    pm = a["attn_persist_mem"]
    ffn = [a["ffn_" + n] for n in ("wf", "wi", "wc", "wo", "uf", "ui", "uc", "uo")]
    arrays = {
        "x": a["attn_x"],
        "x_last": a["attn_x"][:, NT - NEND:NT, :].reshape(NB * NEND, D),
        "w_qkv_t": a["attn_w_qkv"].T,
        "w_out_t": a["attn_w_out"].T,
        "norm_w": a["attn_norm_weight"].reshape(D, 1),
        "pm_k": pm.reshape(NPAIR, 2, NPM, DH).transpose(1, 3, 0, 2).reshape(P, NPAIR * NPM),
        "pm_v": pm.transpose(1, 0, 2).reshape(NPM, DI),
        "ffn_w": np.concatenate([w.T for w in ffn], axis=1),
        "ffn_b": np.stack([a["ffn_" + n] for n in ("bf", "bi", "bc", "in_c")], axis=1),
        "bo_row": a["ffn_bo"].reshape(1, D),
        "consts": constants(),
    }
    arrays = {k: np.ascontiguousarray(v) for k, v in arrays.items()}
    nc = bacc.Bacc("TRN2", target_bir_lowering=False, num_devices=1)
    args = [nc.dram_tensor(k, v.shape, mb.dt.from_np(v.dtype), kind="ExternalInput").ap() for k, v in arrays.items()]
    args.append(nc.dram_tensor("out", (NB, NT, D), mb.dt.float32, kind="ExternalOutput").ap())
    build(nc, *args)
    r = run_bass_kernel_spmd(nc, [arrays], core_ids=[0])
    return r.results[0]["out"]
```

```python
import concourse.bass as bass
from concourse import mybir
from contextlib import ExitStack

NB, NT, D = 32, 256, 128
NH, DH, NPM = 16, 64, 4
DI = NH * DH
P = 128
NPAIR = NH // 2
QT = NT // P
NKEY = NT + NPM
NEND = NKEY - 2 * P
Q1 = P - NPM
QE = NT - NEND
SCOL = NT + (NT - Q1)
CHUNKS = [(0, 0, 0), (1, Q1, NT)]
SW0 = P + NPM
WS = 64.0
RS = 256.0
LOWEST = -3e38
EPS_LN = 1e-5
EPS_RMS = 1.1920928955078125e-07
GATES = 3

CONSTS_F32 = [("ident", P), ("cos", 2 * NT), ("sin", 2 * NT), ("ones_sum", 4 * 32), ("ones_end", 2 * P),
              ("sel_shift_end", NH * NEND)]
CONSTS_CAST = [("sel_shift", NH), ("ident", P), ("mask_q", SW0 + NKEY), ("mask_end", NH * NEND),
               ("sel_pair", NPAIR * P)]


def const_slices(consts):
    at, out = 0, {}
    for name, n in consts:
        out[name] = (at, at + n)
        at += n
    return out, at


def wait(eng, sem, count):
    if isinstance(count, int) and count <= 0:
        return
    eng.wait_ge(sem, count)


def build(nc, x, x_last, w_qkv_t, w_out_t, norm_w, pm_k, pm_v, ffn_w, ffn_b, bo_row, consts_f32, consts_cast,
          out):
    f32, f16, bf16 = mybir.dt.float32, mybir.dt.float16, mybir.dt.bfloat16
    ALU = mybir.AluOpType
    ACT = mybir.ActivationFunctionType
    AX = mybir.AxisListType
    C32, _ = const_slices(CONSTS_F32)
    CS, NCONST = const_slices(CONSTS_CAST)

    ctx = ExitStack()
    with ctx:
        def sb(name, shape, dt):
            return ctx.enter_context(nc.sbuf_tensor(name, shape, dt))

        def sem(name):
            return ctx.enter_context(nc.semaphore(name))

        x_sb = sb("x_sb", [P, NB, QT * D], f32)
        x_end = sb("x_end", [P, D], f32)
        h_hi = sb("h_hi", [P, NKEY], f16)
        h_lo = sb("h_lo", [P, NKEY], f16)
        h_end = sb("h_end", [P, 2, NB * NEND], f16)
        pre = sb("pre", [P, NB, QT * D], f32)
        pre_f = pre[:, :, :].rearrange("p b n -> p (b n)")
        w_raw = pre_f[:, 0:3 * DI]
        f_raw = pre_f[:, 3 * DI:3 * DI + 8 * P]
        c_raw = pre_f[:, 3 * DI + 8 * P:3 * DI + 8 * P + NCONST]
        assert 3 * DI + 8 * P + NCONST <= NB * QT * D
        w_hi = sb("w_hi", [P, 3 * DI], f16)
        w_lo = sb("w_lo", [P, 3 * DI], f16)
        f_hi = sb("f_hi", [P, 8, P], f16)
        f_lo = sb("f_lo", [P, 8, P], f16)
        wo_sb = sb("wo_sb", [P, NPAIR, D], f32)
        cos = sb("cos", [P, 2 * NT], f32)
        sin = sb("sin", [P, 2 * NT], f32)
        ident_f = sb("ident_f", [P, P], f32)
        ident_b = sb("ident_b", [P, P], bf16)
        mask_q = sb("mask_q", [P, SW0 + NKEY], bf16)
        mask_end = sb("mask_end", [P, NH * NEND], bf16)
        sel_pair = sb("sel_pair", [P, NPAIR, P], f16)
        ones_sum = sb("ones_sum", [P, 4, 32], f32)
        ones_end = sb("ones_end", [P, 2, P], f32)
        bias_raw = sb("bias_raw", [P, 4], f32)
        bias_half = sb("bias_half", [P, 2], f32)
        nw = sb("nw", [P, 1], f32)
        bo_sb = sb("bo_sb", [1, D], f32)
        bo_one = sb("bo_one", [1, P], f32)
        pmk_raw = sb("pmk_raw", [P, NPAIR * NPM], f32)
        sh = sb("sh", [P, QT + 1, 6], f32)
        sh_mv = sb("sh_mv", [P, QT + 1, 2], f32)
        sh_u = sb("sh_u", [P, QT + 1], f32)
        sh_r = sb("sh_r", [P, QT + 1], f32)
        expo = sb("expo", [P, QT + 1], f32)
        gate_col = sb("gate_col", [P, NPAIR], f32)
        eps = sb("eps", [P, QT + 1], f32)
        one_e2 = sb("one_e2", [P, QT + 1], f32)
        e1_e2 = sb("e1_e2", [P, QT + 1], f32)
        carry = sb("carry", [P, NH + 3], f32)
        xn0 = sb("xn0", [P, (QT + 1) * D], f32)
        rope_a = sb("rope_a", [P, 4, 2 * NT], f32)
        rope_b = sb("rope_b", [P, 2, 2 * NT], f32)
        qk = sb("qk", [P, NH, 2 * NKEY], f32)
        k_end = sb("k_end", [P, 2, NPAIR * NEND], f32)
        qk_h = sb("qk_h", [P, NPAIR, 2 * NKEY], f16)
        v_sb = sb("v_sb", [P, 2, DI], f32)
        v_end = sb("v_end", [NPAIR * NEND, DI], f32)
        top = sb("top", [P, 2, QT, 2, 64], f32)
        masked = sb("masked", [P, 2, SW0 + NKEY], bf16)
        prob = sb("prob", [P, 4, 2, SCOL], f32)
        prob_add = sb("prob_add", [P, 4, 2, NT - Q1], f32)
        prob_end = sb("prob_end", [NPAIR * NEND, 2, NPAIR, NEND], f32)
        prob_end_sum = sb("prob_end_sum", [NPAIR * NEND, 2, NEND], f32)
        raw = sb("raw", [P, NPAIR, NT], f32)
        linv = sb("linv", [P, NT], f32)
        linv_hi = sb("linv_hi", [P, NT], f16)
        linv_lo = sb("linv_lo", [P, NT], f16)
        sx = sb("sx", [P, QT, 6], f32)
        sx_mv = sb("sx_mv", [P, QT, 2], f32)
        sx_b = sb("sx_b", [P, QT], f32)
        sx_r = sb("sx_r", [P, QT], f32)
        xn = sb("xn", [P, QT * D], f32)
        xt_hi = sb("xt_hi", [P, NT], f16)
        xt_lo = sb("xt_lo", [P, NT], f16)
        th = sb("th", [P, GATES, NT], f32)
        ga = sb("ga", [P, NT], f32)
        gb = sb("gb", [P, NT], f32)
        c2 = sb("c2", [P, NT], f32)
        c_hi = sb("c_hi", [P, NT], f16)
        c_lo = sb("c_lo", [P, NT], f16)
        cf = sb("cf", [P, QT * D], f32)
        v_end_dram = nc.dram_tensor("v_end_scratch", [P, DI], f32, kind="Internal").ap()

        bank = [ctx.enter_context(nc.psum_tensor(f"bank{i}", [P, 512], f32)) for i in range(8)]
        ps_proj = [bank[0], bank[1]]
        ps_st = [bank[2], bank[3]]
        ps_sm = bank[4]
        ps_pv = bank[5]
        ps_sum = bank[6]
        ps_misc = bank[7]

        S = {n: sem(n) for n in (
            "ld_x0 ld_x1 ld_x2 ld_x3 ld_w ld_wv ld_c ld_ident ld_rope ld_ffn ld_small ld_wo v_pm ld_end "
            "casts_act casts_dve casts_pool end_xn end_tr end_hi end_done ve_ready ve_copied ve_stored "
            "h_stats h_rstd h_xn h_tr h_hi_done h_lo_done "
            "qk_proj qk_read rope_mul rope_sum hi_done qk_done sm_ready max_done top_done top_tr top_copied "
            "st_ready exp_done causal_done prob_added pv_ready raw_done sum_ready linv_done r_ready norm_done y_ready x1_done "
            "v_ready v_done v_end sx_done sx_rstd xn_ready xt_ready xt_hi_done xt_lo_done gate_ready gate_read state_done "
            "end_exp end_summed k_end_done cf_ready cf_done fin_sum fin_sum_pool fin_tanh fin_out fin_out_pool stored "
            "dve_pro dve_s dve_h dve_b dve_c pool_h pool_b").split()}

        DVE_H, DVE_B, DVE_C, POOL_H = 1, 2, 1, 2
        SHUF = [i ^ 1 for i in range(32)]
        FIN, FIN_DVE_ADD, FIN_DVE_RES = 8, 6, 5
        FIN_ORDER = (0, 1, 6, 2, 3, 7, 4, 5)
        XCH = (0, 1, 4, NB // 2, NB)
        ld_x = [S[f"ld_x{i}"] for i in range(4)]
        x_d = x.rearrange("b (q p) d -> p b q d", p=P)
        out_d = out.rearrange("b (q p) d -> p b q d", p=P)

        def at3(t, b):
            return t[:, b, :] if isinstance(b, int) else t[:, bass.ds(b, 1), :].rearrange("p o n -> p (o n)")

        def at3s(t, b, lo, hi):
            return t[:, b, lo:hi] if isinstance(b, int) else t[:, bass.ds(b, 1), lo:hi].rearrange("p o n -> p (o n)")

        def iterations(eng, body):
            for j in (0, 1, 2):
                body(j, True, True, j >= 1, j >= 2)
            with eng.Fori(3, NB - 1) as j:
                body(j, True, True, True, True)
            body(NB - 1, False, True, True, True)
            body(NB, False, False, True, True)
            body(NB + 1, False, False, False, True)

        OWN = (slice(0, 64), slice(64, 128))

        def fin_add(eng, g):
            v = pre[:, 4 * g:4 * g + 4, :]
            return eng.tensor_tensor(v, v, cf[:, :].unsqueeze(1).to_broadcast([P, 4, QT * D]), ALU.add)

        def fin_res(eng, g):
            o = x_sb[:, 4 * g:4 * g + 4, :]
            return eng.tensor_tensor(o, o, pre[:, 4 * g:4 * g + 4, :], ALU.add)

        def top_bank(j, h):
            return ps_st[1] if h % 2 and (h > 12 or isinstance(j, int) and j == 0) else ps_sm

        block = ctx.enter_context(nc.Block())

        @block.sync
        def _(sp):
            def const_f32(t, name):
                return sp.dma_start(t, consts_f32[:, C32[name][0]:C32[name][1]])

            def load_x(i):
                lo, hi = XCH[i], XCH[i + 1]
                sp.dma_start(x_sb[:, lo:hi, :].rearrange("p b (q d) -> p b q d", q=QT),
                             x_d[:, lo:hi, :, :]).then_inc(ld_x[i], 16)

            sp.dma_start(x_end[:, :], x_last).then_inc(S["ld_end"], 16)
            load_x(0)
            const_f32(ident_f[:, :], "ident").then_inc(S["ld_ident"], 16)
            sp.dma_start(nw[:, :], norm_w).then_inc(S["ld_ident"], 16)
            sp.dma_start(bias_raw[:, :], ffn_b).then_inc(S["ld_ident"], 16)
            const_f32(cos[:, :], "cos").then_inc(S["ld_rope"], 16)
            const_f32(sin[:, :], "sin").then_inc(S["ld_rope"], 16)
            sp.dma_start(c_raw, consts_cast).then_inc(S["ld_c"], 16)
            sp.dma_start(pmk_raw[:, :], pm_k).then_inc(S["ld_small"], 16)
            sp.dma_start(bo_sb[:, :], bo_row).then_inc(S["ld_small"], 16)
            const_f32(ones_sum[:, :, :].rearrange("p c n -> p (c n)"), "ones_sum").then_inc(S["ld_small"], 16)
            const_f32(ones_end[:, :, :].rearrange("p e n -> p (e n)"), "ones_end").then_inc(S["ld_small"], 16)
            const_f32(k_end[:, :, :].rearrange("p e n -> p (e n)"), "sel_shift_end").then_inc(S["ld_small"], 16)
            load_x(1)
            sp.dma_start(f_raw, ffn_w).then_inc(S["ld_ffn"], 16)
            sp.dma_start(wo_sb[:, :, :], w_out_t.rearrange("(c p) d -> p c d", p=P)).then_inc(S["ld_wo"], 16)
            load_x(2)
            load_x(3)
            sp.wait_ge(S["ve_copied"], 2)
            sp.dma_start(v_end_dram, raw[:, 0:4, :].rearrange("p c n -> p (c n)")).then_inc(S["ve_stored"], 16)
            sp.wait_ge(S["ve_stored"], 16)

            def body(j, h, a, b, c):
                if not a:
                    return
                wait(sp, S["pv_ready"], NPAIR * j)
                src = v_end_dram[NEND * j:NEND * j + NEND, :] if isinstance(j, int) else v_end_dram[bass.ds(j * NEND, NEND), :]
                for s in range(NPAIR):
                    sp.dma_start(v_end[s * NEND:(s + 1) * NEND, :], src).then_inc(S["v_end"], 16)
                sp.wait_ge(S["v_done"], 4 * j + 2)
                sp.dma_start(v_sb[0:NPM, 0, :], pm_v).then_inc(S["v_pm"], 16)

            iterations(nc.sync, body)
            for g in (0, 1, 2, 6, 3, 7, 4, 5):
                if g < FIN_DVE_RES:
                    sp.wait_ge(S["fin_out"], g + 1)
                else:
                    sp.wait_ge(S["fin_out_pool"], (6, 7, 5).index(g) + 1)
                sp.dma_start(out_d[:, 4 * g:4 * g + 4, :, :],
                             x_sb[:, 4 * g:4 * g + 4, :].rearrange("p b (q d) -> p b q d", q=QT)).then_inc(S["stored"], 16)
            sp.wait_ge(S["stored"], 16 * FIN)

        @block.gpsimd
        def _(pool):
            G = nc.gpsimd
            G.memset(expo[:, :], -0.5).then_inc(S["casts_pool"], 1)
            G.memset(top[:, :, :, :, :], 0.0).then_inc(S["casts_pool"], 1)
            G.memset(h_hi[:, 0:NPM], 0.0).then_inc(S["casts_pool"], 1)
            G.memset(h_lo[:, 0:NPM], 0.0).then_inc(S["casts_pool"], 1)
            G.memset(bo_one[:, :], WS).then_inc(S["casts_pool"], 1)
            G.memset(eps[:, :], EPS_LN).then_inc(S["casts_pool"], 1)
            G.memset(one_e2[:, :], 1.0 + EPS_RMS).then_inc(S["casts_pool"], 1)
            G.memset(e1_e2[:, :], EPS_LN * EPS_RMS).then_inc(S["casts_pool"], 1)

            def factors(n, count, base):
                v, u = sh_mv[:, 0:n, 1], sh_u[:, 0:n]
                pool.wait_ge(S["h_stats"], count)
                G.tensor_tensor(u, v, one_e2[:, 0:n], ALU.mult).then_inc(S["pool_h"], 1)
                pool.wait_ge(S["pool_h"], base + 1)
                G.tensor_tensor(u, u, e1_e2[:, 0:n], ALU.add).then_inc(S["pool_h"], 1)
                pool.wait_ge(S["pool_h"], base + 2)
                G.tensor_tensor(sh_r[:, 0:n], u, expo[:, 0:n], ALU.pow).then_inc(S["h_rstd"], 1)

            pool.wait_ge(S["casts_pool"], 8)
            factors(QT + 1, 1, 0)
            pool.wait_ge(S["ld_rope"], 32)

            def causal(bj, s):
                pool.wait_ge(S["exp_done"], NH * bj + 2 * s + 2)
                G.tensor_tensor(gate_col[:, s:s + 1], expo[:, 0:1], expo[:, 0:1], ALU.mult)
                c0 = prob[:, s % 4, :, 0:P]
                c1 = prob[:, s % 4, :, NT:NT + P]
                G.affine_select(out=c0, in_=c0, compare_op=ALU.is_ge, fill=0.0, base=NPM,
                                pattern=[[0, 2], [1, P]], channel_multiplier=-1)
                G.affine_select(out=c1, in_=c1, compare_op=ALU.is_ge, fill=0.0, base=0,
                                pattern=[[0, 2], [1, P]], channel_multiplier=-1).then_inc(S["causal_done"], 1)

            def body(j, h, a, b, c):
                bj, cj = j - 1, j - 2
                for s in range(NPAIR):
                    if a:
                        pool.wait_ge(S["qk_read"], NPAIR * j + s + 1)
                        G.tensor_tensor(rope_b[:, s % 2, :], rope_b[:, s % 2, :], sin[:, :], ALU.mult).then_inc(S["rope_mul"], 1)
                    if b:
                        causal(bj, s)
                    if a:
                        pool.wait_ge(S["rope_mul"], NPAIR * j + s + 1)
                        G.tensor_tensor(rope_a[:, s % 4, :], rope_a[:, s % 4, :], rope_b[:, s % 2, :],
                                        ALU.add).then_inc(S["rope_sum"], 1)
                    if h and s == 3:
                        factors(QT, j + 2, POOL_H * (j + 1))
                    if c and s == 2:
                        pool.wait_ge(S["sx_done"], cj + 1)
                        G.tensor_tensor(sx_b[:, :], sx_mv[:, :, 1], eps[:, 0:QT], ALU.add).then_inc(S["pool_b"], 1)
                        pool.wait_ge(S["pool_b"], cj + 1)
                        G.tensor_tensor(sx_r[:, :], sx_b[:, :], expo[:, 0:QT], ALU.pow).then_inc(S["sx_rstd"], 1)

            iterations(nc.gpsimd, body)

            pool.wait_ge(S["cf_done"], 1)
            for g in range(FIN_DVE_ADD, FIN):
                fin_add(G, g).then_inc(S["fin_sum_pool"], 1)
            pool.wait_ge(S["x1_done"], NB)
            for g in (6, 7, 5):
                pool.wait_ge(S["fin_tanh"], FIN_ORDER.index(g) + 1)
                fin_res(G, g).then_inc(S["fin_out_pool"], 1)

        @block.scalar
        def _(act):
            A = nc.scalar
            act.dma_start(w_raw[:, 0:2 * DI], w_qkv_t[:, 0:2 * DI]).then_inc(S["ld_w"], 16)
            act.dma_start(w_raw[:, 2 * DI:3 * DI], w_qkv_t[:, 2 * DI:3 * DI]).then_inc(S["ld_wv"], 16)

            def cast(ins):
                ins.then_inc(S["casts_act"], 1)

            act.wait_ge(S["ld_ident"], 48)
            cast(A.activation(bias_half[:, :], bias_raw[:, 0:2], ACT.Copy, scale=0.5))
            act.wait_ge(S["ld_w"], 16)
            cast(A.activation(w_hi[:, 0:2 * DI], w_raw[:, 0:2 * DI], ACT.Copy, scale=WS))

            def h_high(count, read=0):
                act.wait_ge(S["h_tr"], count)
                wait(act, S["v_ready"], read)
                A.activation(h_hi[:, NPM:NKEY], ps_st[0][:, 0:NT], ACT.Copy, scale=nw[:, :]).then_inc(S["h_hi_done"], 1)

            h_high(1)
            act.wait_ge(S["end_tr"], 1)
            A.activation(h_end[:, 0, :], ps_sum[:, 0:P], ACT.Copy, scale=nw[:, :]).then_inc(S["end_hi"], 1)
            act.wait_ge(S["ld_wv"], 16)
            cast(A.activation(w_hi[:, 2 * DI:3 * DI], w_raw[:, 2 * DI:3 * DI], ACT.Copy, scale=WS))
            act.wait_ge(S["ld_c"], 16)

            def const(name):
                return c_raw[:, CS[name][0]:CS[name][1]]

            cast(A.copy(qk[:, :, NT:NT + NKEY], const("sel_shift").unsqueeze(2).to_broadcast([P, NH, NKEY])))
            cast(A.copy(ident_b[:, :], const("ident")))
            cast(A.copy(mask_q[:, :], const("mask_q")))
            act.wait_ge(S["ld_small"], 80)
            act.wait_ge(S["casts_act"], 4)
            pk = pmk_raw[:, :].rearrange("p (c n) -> p c n", c=NPAIR)
            for e in range(2):
                cast(A.copy(qk[OWN[e], e::2, NT:NT + NPM], pk[OWN[e], :, :]))
            cast(A.copy(qk_h[:, :, NT:NT + NPM], pk))

            def late_casts():
                cast(A.copy(mask_end[:, :], const("mask_end")))
                cast(A.copy(sel_pair[:, :, :].rearrange("p c n -> p (c n)"), const("sel_pair")))
                act.wait_ge(S["ld_ffn"], 16)
                fr = f_raw.rearrange("p (g n) -> p g n", g=8)
                cast(A.activation(f_hi[:, 0:4, :], fr[:, 0:4, :], ACT.Copy, scale=WS))
                cast(A.activation(f_hi[:, 4:8, :], fr[:, 4:8, :], ACT.Copy, scale=WS / 2))

            def end_values():
                for u in range(2):
                    act.wait_ge(S["ve_ready"], u + 1)
                    A.activation(raw[:, 2 * u:2 * u + 2, :].rearrange("p c n -> p (c n)"), bank[6 + u][:, :], ACT.Copy,
                                 scale=1.0 / WS).then_inc(S["ve_copied"], 1)

            def hi(j, s):
                act.wait_ge(S["rope_sum"], NPAIR * j + s + 1)
                wait(act, S["sm_ready"], NH * (j - 1) + 2 * s + 2)
                A.activation(qk_h[:, s, :].rearrange("p (u n) -> p u n", u=2)[:, :, 0:NT],
                             rope_a[:, s % 4, :].rearrange("p (u n) -> p u n", u=2), ACT.Copy).then_inc(S["hi_done"], 1)

            def full(j, s):
                wait(act, S["st_ready"], NH * (j - 1) + 2 * s + 2)
                if isinstance(j, int) and j == 0 and s == 0:
                    act.wait_ge(S["casts_act"], 9)
                for e in range(2):
                    h, own = 2 * s + e, OWN[e]
                    ins = A.activation(qk[own, h, 0:2 * (NT + NPM)].rearrange("p (u n) -> p u n", u=2)[:, :, 0:NT],
                                       rope_a[own, s % 4, :].rearrange("p (u n) -> p u n", u=2), ACT.Copy)
                ins.then_inc(S["qk_done"], 1)

            def exp(bj, h):
                s = h // 2
                act.wait_ge(S["st_ready"], NH * bj + h + 1)
                if h % 2 == 0:
                    wait(act, S["sum_ready"], 4 * bj + (s - 4) // 2 + 1)
                if h == 2:
                    wait(act, S["pv_ready"], NPAIR * bj)
                    wait(act, S["end_summed"], bj)
                    A.activation(prob_end[:, :, :, :].rearrange("p e s q -> p (e s q)"),
                                 ps_st[0][0:NPAIR * NEND, SCOL:SCOL + NH * NEND], ACT.Exp).then_inc(S["end_exp"], 1)
                A.activation(prob[:, s % 4, h % 2, :], ps_st[h % 2][:, 0:SCOL], ACT.Exp).then_inc(S["exp_done"], 1)

            def spread_top(j, half, parities):
                act.wait_ge(S["top_tr"], 2 * j + half + 1)
                wait(act, S["st_ready"], NH * (j - 1) + NH // 2 * (half + 1))
                o = (ps_misc, ps_sm)[half]
                for e in parities:
                    h0, h1 = NH // 2 * half + e, NH // 2 * (half + 1)
                    ins = A.activation(qk[OWN[1 - e], h0:h1:2, 0:NT],
                                       o[OWN[1 - e], 0:NT].unsqueeze(1).to_broadcast([64, NPAIR // 2, NT]), ACT.Copy)
                if parities[-1] == 1:
                    ins.then_inc(S["top_copied"], 1)

            def raw_copy(bj, s):
                act.wait_ge(S["pv_ready"], NPAIR * bj + s + 1)
                if s == 0:
                    wait(act, S["y_ready"], bj)
                if isinstance(bj, int) and bj == 0 and s == 0:
                    act.wait_ge(S["ve_stored"], 16)
                A.activation(raw[:, s, :], ps_pv[:, 0:NT], ACT.Copy, scale=1.0 / RS).then_inc(S["raw_done"], 1)

            def body(j, h, a, b, c):
                bj, cj = j - 1, j - 2
                for s in range(NPAIR):
                    if a and s == 7:
                        hi(j, s - 1)
                    if b:
                        exp(bj, 2 * s)
                        exp(bj, 2 * s + 1)
                    if c and s == 4:
                        act.wait_ge(S["xt_ready"], cj + 1)
                        wait(act, S["gate_ready"], 2 * cj)
                        A.activation(xt_hi[:, :], ps_misc[:, 0:NT], ACT.Copy).then_inc(S["xt_hi_done"], 1)
                    if a and 1 <= s < 7:
                        hi(j, s - 1)
                    if a and s >= 1:
                        full(j, s - 1)
                    if isinstance(j, int) and j == 0 and s == 4:
                        end_values()
                        late_casts()
                    if c and s == 5:
                        act.wait_ge(S["gate_ready"], 2 * cj + 1)
                        wait(act, S["state_done"], cj)
                        A.activation(th[:, 0, :], ps_misc[:, 0:NT], ACT.Tanh, bias=bias_half[:, 0:1],
                                     scale=0.5 / WS)
                        A.activation(th[:, 1, :], ps_misc[:, NT:2 * NT], ACT.Tanh, bias=bias_half[:, 1:2],
                                     scale=0.5 / WS).then_inc(S["gate_read"], 1)
                        act.wait_ge(S["gate_ready"], 2 * cj + 2)
                        A.activation(th[:, 2, :], ps_proj[0][:, 0:NT], ACT.Tanh, bias=bias_raw[:, 2:3],
                                     scale=1.0 / WS)
                        A.activation(at3(pre, cj), ps_proj[0][:, NT:2 * NT], ACT.Copy).then_inc(S["gate_read"], 1)
                    if b and s >= 1:
                        raw_copy(bj, s - 1)
                    if a and s >= 6:
                        spread_top(j, 0, (s - 6,))
                if a:
                    def value_copy(n):
                        act.wait_ge(S["v_ready"], 4 * j + n + 1)
                        if n == 0:
                            wait(act, S["pv_ready"], NPAIR * j)
                        A.activation(v_sb[:, n // 2, (n % 2) * 512:(n % 2) * 512 + 512], ps_proj[n % 2][:, :], ACT.Copy,
                                     scale=1.0 / WS).then_inc(S["v_done"], 1)
                    hi(j, NPAIR - 1)
                    value_copy(0)
                if b:
                    raw_copy(bj, NPAIR - 1)
                if a:
                    for n in range(1, 4):
                        value_copy(n)
                if h:
                    h_high(j + 2, 4 * j + 4)
                if a:
                    full(j, NPAIR - 1)
                    act.wait_ge(S["qk_done"], NPAIR * j + NPAIR)
                    wait(act, S["st_ready"], NH * (j - 1) + 3)
                    for e in range(2):
                        ins = A.activation(k_end[OWN[e], e, :].rearrange("p (s n) -> p s n", s=NPAIR),
                                           qk[OWN[e], e::2, NKEY + QE:NKEY + NT], ACT.Copy)
                    ins.then_inc(S["k_end_done"], 1)
                    spread_top(j, 1, (0, 1))

            iterations(nc.scalar, body)

            act.wait_ge(S["cf_ready"], 1)
            A.copy(cf[:, :], ps_misc[:, 0:NT]).then_inc(S["cf_done"], 1)
            d, p = 0, 0
            for g in FIN_ORDER:
                if g < FIN_DVE_ADD:
                    d += 1
                    act.wait_ge(S["fin_sum"], d)
                else:
                    p += 1
                    act.wait_ge(S["fin_sum_pool"], p)
                v = pre[:, 4 * g:4 * g + 4, :]
                A.activation(v, v, ACT.Tanh, scale=1.0 / WS).then_inc(S["fin_tanh"], 1)

        @block.vector
        def _(dve):
            V = nc.vector
            chain = [0]

            def link(ins):
                chain[0] += 1
                ins.then_inc(S["dve_pro"], 1)
                dve.wait_ge(S["dve_pro"], chain[0])

            def moments(src, mv, n):
                for q in range(n):
                    last = V.bn_aggr(mv[:, q, :], src[:, q, :])
                return last

            def normalise(q, src):
                return V.tensor_scalar(xn0[:, q * D:(q + 1) * D], src, sh_mv[:, q, 0:1], sh_r[:, q:q + 1],
                                       ALU.subtract, ALU.mult)

            def h_low(count):
                dve.wait_ge(S["h_hi_done"], count)
                V.scalar_tensor_tensor(h_lo[:, NPM:NKEY], ps_st[0][:, 0:NT], nw[:, :], h_hi[:, NPM:NKEY],
                                       ALU.mult, ALU.subtract).then_inc(S["h_lo_done"], 1)

            dve.wait_ge(S["ld_end"], 16)
            V.bn_stats(sh[:, QT, :], x_end[:, :])
            dve.wait_ge(ld_x[0], 16)
            V.bn_stats(sh[:, 0, :], x_sb[:, 0, 0:D])
            link(V.bn_stats(sh[:, 1, :], x_sb[:, 0, D:2 * D]))
            moments(sh, sh_mv, QT + 1).then_inc(S["h_stats"], 1)
            dve.wait_ge(S["h_rstd"], 1)
            for q in range(QT):
                last = normalise(q, x_sb[:, 0, q * D:(q + 1) * D])
            last.then_inc(S["h_xn"], 1)
            normalise(QT, x_end[:, :]).then_inc(S["end_xn"], 1)
            h_low(1)
            dve.wait_ge(S["casts_act"], 2)
            V.scalar_tensor_tensor(w_lo[:, 0:2 * DI], w_raw[:, 0:2 * DI], WS, w_hi[:, 0:2 * DI], ALU.mult,
                                   ALU.subtract).then_inc(S["casts_dve"], 1)
            dve.wait_ge(S["ld_rope"], 32)

            def end_low():
                dve.wait_ge(S["end_hi"], 1)
                V.scalar_tensor_tensor(h_end[:, 1, :], ps_sum[:, 0:P], nw[:, :], h_end[:, 0, :],
                                       ALU.mult, ALU.subtract).then_inc(S["end_done"], 1)
                dve.wait_ge(S["casts_act"], 3)
                V.scalar_tensor_tensor(w_lo[:, 2 * DI:3 * DI], w_raw[:, 2 * DI:3 * DI], WS, w_hi[:, 2 * DI:3 * DI],
                                       ALU.mult, ALU.subtract).then_inc(S["casts_dve"], 1)

            def scan_starts():
                dve.wait_ge(S["casts_act"], 13)
                fr = f_raw.rearrange("p (g n) -> p g n", g=8)
                for u, scale in ((0, WS), (4, WS / 2)):
                    V.scalar_tensor_tensor(f_lo[:, u:u + 4, :], fr[:, u:u + 4, :], scale, f_hi[:, u:u + 4, :], ALU.mult,
                                           ALU.subtract).then_inc(S["casts_dve"], 1)
                link(V.memset(c2[:, :], 2.0))
                link(V.tensor_scalar(c2[:, :], c2[:, :], bias_raw[:, 3:4], None, ALU.mult))
                link(V.tensor_copy(c_hi[:, :], c2[:, :]))
                link(V.tensor_tensor(c_lo[:, :], c2[:, :], c_hi[:, :], ALU.subtract))

            def body(j, h, a, b, c):
                bj, cj = j - 1, j - 2
                kh, kb, kc = [0], [0], [0]

                def carry_wait(column):
                    V.tensor_tensor(carry[:, column:column + 1], expo[:, 0:1], expo[:, 0:1], ALU.mult)

                def link_h(ins):
                    kh[0] += 1
                    ins.then_inc(S["dve_h"], 1)
                    dve.wait_ge(S["dve_h"], DVE_H * j + kh[0])

                def link_b(ins):
                    kb[0] += 1
                    ins.then_inc(S["dve_b"], 1)
                    dve.wait_ge(S["dve_b"], DVE_B * bj + kb[0])

                def link_c(ins):
                    kc[0] += 1
                    ins.then_inc(S["dve_c"], 1)
                    dve.wait_ge(S["dve_c"], DVE_C * cj + kc[0])

                def maxima(h):
                    dve.wait_ge(S["sm_ready"], NH * j + h + 1)
                    if h in (0, NH // 2):
                        wait(dve, S["top_tr"], 2 * (j - 1) + 1 + h // (NH // 2))
                        if isinstance(j, int) and j == 0:
                            dve.wait_ge(S["casts_pool"], 2)
                    carry_wait(h)
                    for q, c0, n in ((0, 0, SW0), (1, SW0, NKEY)):
                        ins = V.tensor_tensor_reduce(masked[:, h % 2, c0:c0 + n], top_bank(j, h)[:, c0:c0 + n], mask_q[:, c0:c0 + n], 1.0,
                                                     LOWEST, ALU.add, ALU.max, top[:, h // 8, q, 0, h:h + 1])
                    ins.then_inc(S["max_done"], 1)

                def copy_top(half):
                    n = NH // 2
                    dve.wait_ge(S["max_done"], NH * j + n * (half + 1))
                    V.tensor_copy(top[:, half, :, 1, n * half:n * half + n],
                                  top[:, half, :, 0, n * half:n * half + n]).then_inc(S["top_done"], 1)

                def add_chunks(s):
                    dve.wait_ge(S["causal_done"], NPAIR * bj + s + 1)
                    wait(dve, S["sum_ready"], 4 * bj + (s - 4) // 2 + 1)
                    V.tensor_tensor(prob_add[:, s % 4, :, :], prob[:, s % 4, :, Q1:NT], prob[:, s % 4, :, NT:SCOL],
                                    ALU.add).then_inc(S["prob_added"], 1)

                def divide(n):
                    dve.wait_ge(S["r_ready"], 4 * cj + n + 1)
                    if n == 0:
                        dve.wait_ge(S["raw_done"], NPAIR * cj + NPAIR)
                    r = (ps_pv, ps_sum)[n % 2]
                    o = raw[:, 2 * n:2 * n + 2, :].rearrange("p c n -> p (c n)")
                    V.tensor_tensor(o, r[:, :], o, ALU.mult).then_inc(S["norm_done"], 1)

                for s in range(NPAIR):
                    if isinstance(j, int) and j == 0:
                        if s == 1:
                            end_low()
                        if s == 6:
                            scan_starts()
                    if a:
                        if s >= 2 and b:
                            maxima(2 * s - 4)
                        dve.wait_ge(S["qk_proj"], NPAIR * j + s + 1)
                        wait(dve, S["qk_done"], NPAIR * j + s - 3)
                        wait(dve, S["rope_sum"], NPAIR * j + s - 1)
                        V.tensor_tensor(rope_a[:, s % 4, :], ps_proj[s % 2][:, :], cos[:, :], ALU.mult)
                        V.stream_shuffle(rope_b[:, s % 2, :], ps_proj[s % 2][:, :], SHUF).then_inc(S["qk_read"], 1)
                        if s >= 2 and not b:
                            maxima(2 * s - 4)
                    if b and s == 2:
                        dve.wait_ge(S["end_exp"], bj + 1)
                        wait(dve, S["sum_ready"], 4 * bj)
                        V.tensor_reduce(prob_end_sum[:, :, :], prob_end[:, :, :, :].rearrange("p e s q -> p e q s"), AX.X,
                                        ALU.add).then_inc(S["end_summed"], 1)
                    if c and s <= 1:
                        divide(2 * s)
                        divide(2 * s + 1)
                    if a and s >= 2:
                        maxima(2 * s - 3)
                    if c and s == 3:
                        dve.wait_ge(S["sx_rstd"], cj + 1)
                        wait(dve, S["xt_ready"], cj)
                        for q in range(QT):
                            last = V.tensor_scalar(xn[:, q * D:(q + 1) * D], at3s(x_sb, cj, q * D, (q + 1) * D),
                                                   sx_mv[:, q, 0:1], sx_r[:, q:q + 1], ALU.subtract, ALU.mult)
                        last.then_inc(S["xn_ready"], 1)
                    if a and s == 5:
                        copy_top(0)
                    if h and s == 0:
                        if isinstance(j, int):
                            for i in range(1, 4):
                                if j == (0 if i == 1 else 2):
                                    dve.wait_ge(ld_x[i], 16)
                        dve.wait_ge(S["h_xn"], j + 1)
                        V.bn_stats(sh[:, 0, :], at3s(x_sb, j + 1, 0, D))
                        link_h(V.bn_stats(sh[:, 1, :], at3s(x_sb, j + 1, D, 2 * D)))
                        carry_wait(NH + 2)
                        moments(sh, sh_mv, QT).then_inc(S["h_stats"], 1)
                    if b and s >= 1:
                        add_chunks(s - 1)
                    if c and s == 1:
                        dve.wait_ge(S["y_ready"], cj + 1)
                        V.tensor_tensor(at3(x_sb, cj), ps_misc[:, 0:QT * D], at3(x_sb, cj), ALU.add).then_inc(S["x1_done"], 1)
                        dve.wait_ge(S["x1_done"], cj + 1)
                        carry_wait(NH)
                        V.bn_stats(sx[:, 0, :], at3s(x_sb, cj, 0, D))
                        link_c(V.bn_stats(sx[:, 1, :], at3s(x_sb, cj, D, 2 * D)))
                        carry_wait(NH + 1)
                        moments(sx, sx_mv, QT).then_inc(S["sx_done"], 1)
                    if h and s == 6:
                        dve.wait_ge(S["h_rstd"], j + 2)
                        dve.wait_ge(S["h_tr"], j + 1)
                        for q in range(QT):
                            last = normalise(q, at3s(x_sb, j + 1, q * D, (q + 1) * D))
                        last.then_inc(S["h_xn"], 1)
                    if c and s == 4:
                        dve.wait_ge(S["xt_hi_done"], cj + 1)
                        V.tensor_tensor(xt_lo[:, :], ps_misc[:, 0:NT], xt_hi[:, :], ALU.subtract).then_inc(S["xt_lo_done"], 1)
                    if c and s == 6:
                        dve.wait_ge(S["gate_read"], 2 * cj + 2)
                        V.scalar_tensor_tensor(ga[:, :], th[:, 0, :], 1.0, c2[:, :], ALU.add, ALU.mult).then_inc(S["dve_s"], 1)
                        V.scalar_tensor_tensor(gb[:, :], th[:, 1, :], 1.0, th[:, 2, :], ALU.add, ALU.mult).then_inc(S["dve_s"], 1)
                    if c and s == 7:
                        dve.wait_ge(S["dve_s"], 4 * cj + 2)
                        V.scalar_tensor_tensor(c2[:, :], ga[:, :], 0.5, gb[:, :], ALU.mult, ALU.add).then_inc(S["dve_s"], 1)
                if a:
                    maxima(12)
                if c:
                    dve.wait_ge(S["dve_s"], 4 * cj + 3)
                    V.tensor_copy(c_hi[:, :], c2[:, :]).then_inc(S["dve_s"], 1)
                if a:
                    maxima(13)
                if c:
                    dve.wait_ge(S["dve_s"], 4 * cj + 4)
                    V.tensor_tensor(c_lo[:, :], c2[:, :], c_hi[:, :], ALU.subtract).then_inc(S["state_done"], 1)
                if b:
                    add_chunks(NPAIR - 1)
                if a:
                    maxima(14)
                    maxima(15)
                    copy_top(1)
                if h:
                    h_low(j + 2)
                if b:
                    dve.wait_ge(S["sum_ready"], 4 * bj + 4)
                    link_b(V.reciprocal(linv[:, :], ps_sum[:, 0:NT]))
                    link_b(V.tensor_copy(linv_hi[:, :], linv[:, :]))
                    V.tensor_tensor(linv_lo[:, :], linv[:, :], linv_hi[:, :], ALU.subtract).then_inc(S["linv_done"], 1)
                assert not h or kh[0] == DVE_H
                assert not b or kb[0] == DVE_B
                assert not c or kc[0] == DVE_C

            iterations(nc.vector, body)

            dve.wait_ge(S["cf_done"], 1)
            for g in range(FIN_DVE_ADD):
                fin_add(V, g).then_inc(S["fin_sum"], 1)
                if g >= 2:
                    dve.wait_ge(S["fin_tanh"], FIN_ORDER.index(g - 2) + 1)
                    fin_res(V, g - 2).then_inc(S["fin_out"], 1)
            for g in range(FIN_DVE_ADD - 2, FIN_DVE_RES):
                dve.wait_ge(S["fin_tanh"], FIN_ORDER.index(g) + 1)
                fin_res(V, g).then_inc(S["fin_out"], 1)

        @block.tensor
        def _(pe):
            T = nc.tensor
            pe.wait_ge(S["ld_ident"], 48)

            def transpose_x(j):
                pe.wait_ge(S["h_xn"], j + 1)
                for q in range(QT):
                    last = T.transpose(ps_st[0][:, q * P:(q + 1) * P], xn0[:, q * D:(q + 1) * D], ident_f[:, :])
                last.then_inc(S["h_tr"], 1)

            transpose_x(0)
            pe.wait_ge(S["end_xn"], 1)
            T.transpose(ps_sum[:, 0:P], xn0[:, QT * D:(QT + 1) * D], ident_f[:, :]).then_inc(S["end_tr"], 1)
            SPLIT = [(0, 0), (0, 1), (1, 0)]
            H, W, FW = (h_hi, h_lo), (w_hi, w_lo), (f_hi, f_lo)
            pe.wait_ge(S["casts_dve"], 1)

            def end_values():
                pe.wait_ge(S["end_done"], 1)
                pe.wait_ge(S["casts_dve"], 2)
                for u in range(2):
                    for i, (p, q) in enumerate(SPLIT):
                        last = T.matmul(bank[6 + u][:, :], h_end[:, p, :], W[q][:, 2 * DI + u * 512:2 * DI + u * 512 + 512],
                                        start=(i == 0), stop=(i == 2))
                    last.then_inc(S["ve_ready"], 1)

            def project(j, s):
                if s == 0:
                    pe.wait_ge(S["h_lo_done"], j + 1)
                if s >= 2:
                    pe.wait_ge(S["qk_read"], NPAIR * j + s - 1)
                else:
                    wait(pe, S["v_done"], 4 * j - 1 + s)
                for u in range(2):
                    col = u * DI + s * P
                    for i, (p, q) in enumerate(SPLIT):
                        last = T.matmul(ps_proj[s % 2][:, u * NT:(u + 1) * NT], W[q][:, col:col + P],
                                        H[p][:, NPM:NKEY], start=(i == 0), stop=(i == 2))
                last.then_inc(S["qk_proj"], 1)

            def values(j, n):
                if n < 2:
                    pe.wait_ge(S["qk_read"], NPAIR * j + 7 + n)
                else:
                    pe.wait_ge(S["v_done"], 4 * j + n - 1)
                kc, col = n // 2, 2 * DI + (n % 2) * 512
                for i, (p, q) in enumerate(SPLIT):
                    last = T.matmul(ps_proj[n % 2][:, :], H[p][:, kc * P:kc * P + P], W[q][:, col:col + 512],
                                    start=(i == 0), stop=(i == 2))
                last.then_inc(S["v_ready"], 1)

            def scores_for_max(j, h):
                s, e = h // 2, h % 2
                if e == 0:
                    pe.wait_ge(S["hi_done"], NPAIR * j + s + 1)
                ps = top_bank(j, h)
                two_banks = h > 12 or isinstance(j, int) and j == 0
                wait(pe, S["max_done"], NH * j + h - (1 if two_banks else 0))
                if h == 13:
                    wait(pe, S["exp_done"], NH * (j - 1) + NH)
                if h == 0:
                    wait(pe, S["top_copied"], 2 * j)
                for q, c0, n in ((0, 0, SW0), (1, SW0, NKEY)):
                    last = T.matmul(ps[:, c0:c0 + n], qk_h[OWN[e], s, q * P:(q + 1) * P], qk_h[OWN[e], s, NT:NT + n],
                                    start=True, stop=True)
                last.then_inc(S["sm_ready"], 1)

            def transpose_top(j, half):
                pe.wait_ge(S["top_done"], 2 * j + half + 1)
                if half == 0:
                    wait(pe, S["gate_read"], 2 * (j - 2) + 1)
                o = (ps_misc, ps_sm)[half]
                for q in range(QT):
                    last = T.transpose(o[:, q * P:(q + 1) * P], top[:, half, q, :, :].rearrange("p a b -> p (a b)"),
                                       ident_f[:, :])
                last.then_inc(S["top_tr"], 1)

            def scores_t(bj, h):
                s, e = h // 2, h % 2
                if isinstance(bj, int) and bj == 0 and h == 0:
                    pe.wait_ge(S["ld_small"], 80)
                    pe.wait_ge(S["ld_wo"], 16)
                if h == 0:
                    pe.wait_ge(S["top_copied"], 2 * bj + 1)
                if h == 2:
                    pe.wait_ge(S["top_copied"], 2 * bj + 2)
                if e == 0:
                    pe.wait_ge(S["qk_done"], NPAIR * bj + s + 1)
                wait(pe, S["exp_done"], NH * bj + h - 1)
                ps = ps_st[e]
                for kc, q0, c0 in CHUNKS:
                    last = T.matmul(ps[:, c0:c0 + NT - q0], qk[:, h, NT + kc * P:NT + (kc + 1) * P], qk[:, h, q0:NT],
                                    start=True, stop=True)
                if h == 2:
                    pe.wait_ge(S["k_end_done"], bj + 1)
                    n = NPAIR * NEND
                    for e in range(2):
                        o = ps[0:n, SCOL + e * n:SCOL + (e + 1) * n]
                        T.matmul(o, k_end[:, e, :], qk[:, e::2, QE:NT], start=True, stop=False)
                        last = T.matmul(o, ident_b[:, 0:n], mask_end[:, e * n:(e + 1) * n], start=False, stop=True)
                last.then_inc(S["st_ready"], 1)

            def attend(bj, s):
                pe.wait_ge(S["causal_done"], NPAIR * bj + s + 1)
                wait(pe, S["raw_done"], NPAIR * bj + s)
                if s == 0:
                    pe.wait_ge(S["v_done"], 4 * bj + 4)
                    pe.wait_ge(S["v_end"], 16 * NPAIR * (bj + 1))
                    pe.wait_ge(S["v_pm"], 16 * (bj + 1))
                    pe.wait_ge(S["end_exp"], bj + 1)
                    wait(pe, S["norm_done"], 4 * bj)
                for kc, q0, c0 in CHUNKS:
                    for e in range(2):
                        col = (2 * s + e) * DH
                        T.matmul(ps_pv[64 * e:64 * e + 64, q0:NT], v_sb[:, kc, col:col + DH],
                                 prob[:, s % 4, e, c0:c0 + NT - q0], start=(kc == 0), stop=False)
                for e in range(2):
                    col = (2 * s + e) * DH
                    last = T.matmul(ps_pv[64 * e:64 * e + 64, QE:NT], v_end[:, col:col + DH], prob_end[:, e, s, :],
                                    start=False, stop=True)
                last.then_inc(S["pv_ready"], 1)

            def sums(bj, g):
                pe.wait_ge(S["prob_added"], NPAIR * bj + 2 * g + 2)
                for part, cols in ((0, slice(0, Q1)), (1, slice(Q1, NT))):
                    for r in range(4):
                        slot = (2 * g + r // 2) % 4
                        p = prob[:, slot, r % 2, cols] if part == 0 else prob_add[:, slot, r % 2, :]
                        last = T.matmul(ps_sum[32 * r:32 * r + 32, cols], ones_sum[:, g, :], p,
                                        start=(g == 0 and part == 0), stop=False, skip_group_check=True)
                if g == 3:
                    pe.wait_ge(S["end_summed"], bj + 1)
                    for e in range(2):
                        last = T.matmul(ps_sum[:, QE:NT], ones_end[0:NPAIR * NEND, e, :], prob_end_sum[:, e, :],
                                        start=False, stop=(e == 1), skip_group_check=True)
                last.then_inc(S["sum_ready"], 1)

            def spread(bj, n):
                if n == 0:
                    pe.wait_ge(S["linv_done"], bj + 1)
                    pe.wait_ge(S["raw_done"], NPAIR * bj + NPAIR)
                if n >= 2:
                    pe.wait_ge(S["norm_done"], 4 * bj + n - 1)
                r = (ps_pv, ps_sum)[n % 2]
                for u in range(2):
                    T.matmul(r[:, u * NT:(u + 1) * NT], sel_pair[:, 2 * n + u, :], linv_hi[:, :], start=True, stop=False)
                    last = T.matmul(r[:, u * NT:(u + 1) * NT], sel_pair[:, 2 * n + u, :], linv_lo[:, :],
                                    start=False, stop=True)
                last.then_inc(S["r_ready"], 1)

            def project_out(bj, n, b):
                pe.wait_ge(S["norm_done"], 4 * bj + n + 1)
                if n == 0 and b:
                    pe.wait_ge(S["top_copied"], 2 * (bj + 1) + 1)
                for s in (2 * n, 2 * n + 1):
                    for q in range(QT):
                        last = T.matmul(ps_misc[:, q * D:(q + 1) * D], raw[:, s, q * P:(q + 1) * P], wo_sb[:, s, :],
                                        start=(s == 0 and q == 0), stop=(s == NPAIR - 1 and q == QT - 1),
                                        skip_group_check=True)
                if n == 3:
                    last.then_inc(S["y_ready"], 1)

            def transpose_xn(cj):
                pe.wait_ge(S["xn_ready"], cj + 1)
                for q in range(QT):
                    last = T.transpose(ps_misc[:, q * P:(q + 1) * P], xn[:, q * D:(q + 1) * D], ident_f[:, :])
                last.then_inc(S["xt_ready"], 1)

            def gates(j, cj, a):
                pe.wait_ge(S["xt_lo_done"], cj + 1)
                wait(pe, S["state_done"], cj)
                X, C = (xt_hi, xt_lo), (c_hi, c_lo)
                if a:
                    pe.wait_ge(S["qk_read"], NPAIR * j + 5)
                for g in range(GATES):
                    o = (ps_misc, ps_proj[0])[g // 2][:, (g % 2) * NT:(g % 2) * NT + NT]
                    for i, (p, q) in enumerate(SPLIT):
                        T.matmul(o, FW[q][:, g, :], X[p][:, :], start=(i == 0), stop=False)
                    for i, (p, q) in enumerate(SPLIT):
                        last = T.matmul(o, FW[q][:, 4 + g, :], C[p][:, :], start=False, stop=(i == 2))
                    if g == 1:
                        last.then_inc(S["gate_ready"], 1)
                for t in range(QT):
                    for i, (p, q) in enumerate(SPLIT):
                        last = T.matmul(ps_proj[0][:, NT + t * D:NT + (t + 1) * D], X[p][:, t * P:(t + 1) * P],
                                        FW[q][:, 3, :], start=(i == 0), stop=(i == 2))
                last.then_inc(S["gate_ready"], 1)

            def body(j, h, a, b, c):
                bj, cj = j - 1, j - 2
                for s in range(NPAIR):
                    if a and s >= 2 and b:
                        scores_for_max(j, 2 * s - 4)
                    if a:
                        if c and s == 6:
                            pe.wait_ge(S["gate_read"], 2 * cj + 2)
                        project(j, s)
                    if c and s == 4:
                        transpose_xn(cj)
                    if isinstance(j, int) and j == 0 and s == 3:
                        end_values()
                    if a and s >= 2 and not b:
                        scores_for_max(j, 2 * s - 4)
                    if c and s == 1:
                        spread(cj, 0)
                        spread(cj, 1)
                    if b:
                        scores_t(bj, 2 * s)
                    if c and s == 1:
                        project_out(cj, 0, b)
                        spread(cj, 2)
                    if a and s >= 2:
                        scores_for_max(j, 2 * s - 3)
                    if b:
                        scores_t(bj, 2 * s + 1)
                    if a and s == 6:
                        transpose_top(j, 0)
                    if c and s == 1:
                        project_out(cj, 1, b)
                        spread(cj, 3)
                        project_out(cj, 2, b)
                        project_out(cj, 3, b)
                    if c and s == 5:
                        gates(j, cj, a)
                    if b and s >= 1:
                        attend(bj, s - 1)
                        if s in (3, 5, 7):
                            sums(bj, (s - 3) // 2)
                if isinstance(j, int) and j == 0:
                    pe.wait_ge(S["casts_pool"], 8)
                    pe.wait_ge(S["casts_act"], 13)
                    pe.wait_ge(S["ve_copied"], 2)
                if isinstance(j, int) and j == 1:
                    pe.wait_ge(S["casts_dve"], 4)
                for n in range(4):
                    if a:
                        scores_for_max(j, 12 + n)
                        values(j, n)
                    if b and n == 0:
                        attend(bj, NPAIR - 1)
                if h:
                    wait(pe, S["exp_done"], NH * bj + NH - 1)
                    transpose_x(j + 1)
                if b:
                    sums(bj, 3)
                if a:
                    transpose_top(j, 1)

            iterations(nc.tensor, body)

            pe.wait_ge(S["state_done"], NB)
            C = (c_hi, c_lo)
            for t in range(QT):
                o = ps_misc[:, t * D:(t + 1) * D]
                for i, (p, q) in enumerate(SPLIT):
                    T.matmul(o, C[p][:, t * P:(t + 1) * P], FW[q][:, 7, :], start=(i == 0), stop=False)
                last = T.matmul(o, bo_one[:, :], bo_sb[:, :], start=False, stop=True)
            last.then_inc(S["cf_ready"], 1)


def constants():
    import numpy as np
    packed = []
    for consts in (CONSTS_F32, CONSTS_CAST):
        cols, n = const_slices(consts)
        packed.append((cols, np.zeros((P, n), np.float32)))

    def put(name, a):
        for cols, c in packed:
            if name in cols:
                c[:a.shape[0], cols[name][0]:cols[name][1]] = a

    f = np.arange(0, DH, 2, dtype=np.float32) / np.float32(DH)
    inv = (np.float32(1.0) / np.power(np.float32(10000.0), f)).astype(np.float32)
    ang = np.arange(NT, dtype=np.float32)[:, None] * inv[None, :]
    ang = np.repeat(ang, 2, axis=1).T
    sign = np.where(np.arange(DH) % 2 == 0, -1.0, 1.0).astype(np.float32)[:, None]
    both = np.array([DH ** -0.5, 1.0], np.float32) / np.float32(WS)
    put("cos", np.concatenate([np.tile(np.cos(ang), (2, 1)) * f for f in both], axis=1))
    put("sin", np.concatenate([np.tile(np.sin(ang) * sign, (2, 1)) * f for f in both], axis=1))
    put("ident", np.eye(P, dtype=np.float32))
    p = np.arange(P)[:, None]
    mask = np.zeros((P, SW0 + NKEY))
    mask[:, 0:SW0] = np.where(np.arange(SW0)[None, :] > p + NPM, -1e30, 0.0)
    mask[:, SW0 + P:] = mask[:, 0:SW0]
    put("mask_q", mask)
    n = NPAIR * NEND
    row, col = np.arange(n)[:, None], np.arange(n)[None, :]
    own = (row // NEND == col // NEND) & (row % NEND <= col % NEND)
    put("mask_end", np.tile(np.where(own, 0.0, -1e30), (1, 2)))
    sel = np.zeros((P, NPAIR, P))
    shift, shift_end, ones_end = np.zeros((P, NH)), np.zeros((P, 2, n)), np.zeros((P, 2, P))
    for h in range(NH):
        sel[32 * (h % 4) + h // 4, h // 2, 64 * (h % 2):64 * (h % 2) + 64] = 1.0
        s, e = h // 2, h % 2
        shift[64 * (1 - e) + h, h] = -1.0
        shift_end[64 * (1 - e) + h, e, s * NEND:(s + 1) * NEND] = -1.0
        ones_end[s * NEND:(s + 1) * NEND, e, 32 * (h % 4) + h // 4:32 * (h % 4) + 32:4] = 1.0 / RS
    put("sel_pair", sel.reshape(P, -1))
    put("sel_shift", shift)
    put("sel_shift_end", shift_end.reshape(P, -1))
    put("ones_end", ones_end.reshape(P, -1))
    ones = np.zeros((P, 4, 32))
    for g in range(4):
        ones[:, g, g::4] = 1.0 / RS
    put("ones_sum", ones.reshape(P, -1))
    return [c for _, c in packed]


def kernel(**inputs):
    import numpy as np
    import concourse.bacc as bacc
    from concourse import mybir as mb
    from concourse.bass_utils import run_bass_kernel_spmd

    a = {k[3:]: np.asarray(v) for k, v in inputs.items()}
    pm = a["attn_persist_mem"]
    c_f32, c_cast = constants()
    ffn = [a["ffn_" + n] for n in ("wf", "wi", "wc", "wo", "uf", "ui", "uc", "uo")]
    arrays = {
        "x": a["attn_x"],
        "x_last": a["attn_x"][:, NT - NEND:NT, :].reshape(NB * NEND, D),
        "w_qkv_t": a["attn_w_qkv"].T,
        "w_out_t": a["attn_w_out"].T,
        "norm_w": a["attn_norm_weight"].reshape(D, 1),
        "pm_k": pm.reshape(NPAIR, 2, NPM, DH).transpose(1, 3, 0, 2).reshape(P, NPAIR * NPM),
        "pm_v": pm.transpose(1, 0, 2).reshape(NPM, DI),
        "ffn_w": np.concatenate([w.T for w in ffn], axis=1),
        "ffn_b": np.stack([a["ffn_" + n] for n in ("bf", "bi", "bc", "in_c")], axis=1),
        "bo_row": a["ffn_bo"].reshape(1, D),
        "consts_f32": c_f32,
        "consts_cast": c_cast,
    }
    arrays = {k: np.ascontiguousarray(v) for k, v in arrays.items()}
    nc = bacc.Bacc("TRN2", target_bir_lowering=False, num_devices=1)
    args = [nc.dram_tensor(k, v.shape, mb.dt.from_np(v.dtype), kind="ExternalInput").ap() for k, v in arrays.items()]
    args.append(nc.dram_tensor("out", (NB, NT, D), mb.dt.float32, kind="ExternalOutput").ap())
    build(nc, *args)
    r = run_bass_kernel_spmd(nc, [arrays], core_ids=[0])
    return r.results[0]["out"]
```
